# Optimizing a Trainium2 kernel written in Bass

```python
import numpy as np
import jax
import jax.numpy as jnp

def _softmax(x, axis=-1):
    return jax.nn.softmax(x, axis=axis)

def _gelu(x):
    return jax.nn.gelu(x, approximate=True)

def _silu(x):
    return jax.nn.silu(x)

def _sigmoid(x):
    return jax.nn.sigmoid(x)

def _layernorm(x, axis=-1, eps=1e-05):
    m = jnp.mean(x, axis=axis, keepdims=True)
    v = jnp.var(x, axis=axis, keepdims=True)
    return (x - m) / jnp.sqrt(v + eps)

def _scatter_add(tgt, idx, src, axis=0):
    return tgt.at[idx].add(src)

def _segment_sum(src, seg, n):
    return jax.ops.segment_sum(src, seg, n)
kernel_name = 'mk_seq_postln_d1_jaxref_r4_6437a6'

def setup_inputs(seed: int=0):
    np.random.seed(seed)
    _w = jnp.asarray

    def _L0_attn_setup():
        import jax, jax.numpy as jnp
        import numpy as np
        B, T, C = (8, 512, 256)
        HS = 64
        H = C // HS
        LORA_R = 32
        TD_R = 64

        def _wkv6(r, k, v, w, u):
            n = r.shape[-1]
            decay = jnp.exp(-jnp.exp(w))

            def per_head(rt, kt, vt, dt, uh):

                def step(S, inp):
                    ri, ki, vi, di = inp
                    kv = ki[:, None] * vi[None, :]
                    y = ri @ (S + uh[:, None] * kv)
                    S = di[:, None] * S + kv
                    return (S, y)
                S0 = jnp.zeros((n, n), rt.dtype)
                _, ys = jax.lax.scan(step, S0, (rt, kt, vt, dt))
                return ys
            f = jax.vmap(per_head, in_axes=(0, 0, 0, 0, 0))
            f = jax.vmap(f, in_axes=(0, 0, 0, 0, None))
            return f(r, k, v, decay, u)
        key = jax.random.key(seed)
        ks = jax.random.split(key, 20)
        inp = {'x': jax.random.normal(ks[0], (B, T, C), jnp.float32), 'miu_x': jax.random.uniform(ks[1], (1, 1, C), jnp.float32), 'lambda_': jax.random.uniform(ks[2], (5, 1, 1, C), jnp.float32), 'A_lora': jax.random.normal(ks[3], (C, LORA_R * 5), jnp.float32) * 0.01, 'B_lora': jax.random.normal(ks[4], (5, LORA_R, C), jnp.float32) * 0.01, 'td_miu': -6.0 + 5.0 * jax.random.uniform(ks[5], (1, 1, C), jnp.float32), 'td_A': jax.random.normal(ks[6], (C, TD_R), jnp.float32) * 0.01, 'td_B': jax.random.normal(ks[7], (TD_R, C), jnp.float32) * 0.01, 'u': jax.random.normal(ks[8], (H, HS), jnp.float32) * 0.1, 'Wr': jax.random.normal(ks[9], (C, C), jnp.float32) * 0.02, 'Wk': jax.random.normal(ks[10], (C, C), jnp.float32) * 0.02, 'Wv': jax.random.normal(ks[11], (C, C), jnp.float32) * 0.02, 'Wg': jax.random.normal(ks[12], (C, C), jnp.float32) * 0.02, 'Wo': jax.random.normal(ks[13], (C, C), jnp.float32) * 0.02, 'gn_gamma': jnp.ones((C,), jnp.float32), 'gn_beta': jnp.zeros((C,), jnp.float32)}
        return inp
    _L0_attn_in = _L0_attn_setup()

    def _L0_ffn_setup():
        import jax, jax.numpy as jnp
        import numpy as np
        S, B, D = (256, 2, 256)
        E, TOPK = (15, 3)
        F = 256
        FS = 512

        def _uinit(k, shape, out_dim):
            std = out_dim ** (-0.5)
            return jax.random.uniform(k, shape, jnp.float32, -std, std)
        key = jax.random.key(seed)
        ks = jax.random.split(key, 10)
        return {'x': jax.random.normal(ks[0], (S, B, D), jnp.float32), 'gate_w': jax.random.normal(ks[1], (E, D), jnp.float32) * D ** (-0.5), 'fc1_w': _uinit(ks[2], (E, 2 * F, D), 2 * F), 'fc1_b': _uinit(ks[3], (E, 2 * F), 2 * F), 'geglu_mult': jnp.ones((E, F), jnp.float32), 'fc2_w': _uinit(ks[4], (E, D, F), D), 'fc2_b': _uinit(ks[5], (E, D), D), 's_fc1_w': _uinit(ks[6], (2 * FS, D), 2 * FS), 's_fc1_b': _uinit(ks[7], (2 * FS,), 2 * FS), 's_geglu_mult': jnp.ones((FS,), jnp.float32), 's_fc2_w': _uinit(ks[8], (D, FS), D), 's_fc2_b': _uinit(ks[9], (D,), D)}
    _L0_ffn_in = _L0_ffn_setup()
    _d = {'L0_attn_x': _L0_attn_in['x'], 'L0_attn_miu_x': _L0_attn_in['miu_x'], 'L0_attn_lambda_': _L0_attn_in['lambda_'], 'L0_attn_A_lora': _L0_attn_in['A_lora'], 'L0_attn_B_lora': _L0_attn_in['B_lora'], 'L0_attn_td_miu': _L0_attn_in['td_miu'], 'L0_attn_td_A': _L0_attn_in['td_A'], 'L0_attn_td_B': _L0_attn_in['td_B'], 'L0_attn_u': _L0_attn_in['u'], 'L0_attn_Wr': _L0_attn_in['Wr'], 'L0_attn_Wk': _L0_attn_in['Wk'], 'L0_attn_Wv': _L0_attn_in['Wv'], 'L0_attn_Wg': _L0_attn_in['Wg'], 'L0_attn_Wo': _L0_attn_in['Wo'], 'L0_attn_gn_gamma': _L0_attn_in['gn_gamma'], 'L0_attn_gn_beta': _L0_attn_in['gn_beta'], 'L0_ffn_gate_w': _L0_ffn_in['gate_w'], 'L0_ffn_fc1_w': _L0_ffn_in['fc1_w'], 'L0_ffn_fc1_b': _L0_ffn_in['fc1_b'], 'L0_ffn_geglu_mult': _L0_ffn_in['geglu_mult'], 'L0_ffn_fc2_w': _L0_ffn_in['fc2_w'], 'L0_ffn_fc2_b': _L0_ffn_in['fc2_b'], 'L0_ffn_s_fc1_w': _L0_ffn_in['s_fc1_w'], 'L0_ffn_s_fc1_b': _L0_ffn_in['s_fc1_b'], 'L0_ffn_s_geglu_mult': _L0_ffn_in['s_geglu_mult'], 'L0_ffn_s_fc2_w': _L0_ffn_in['s_fc2_w'], 'L0_ffn_s_fc2_b': _L0_ffn_in['s_fc2_b']}
    _x0 = _d['L0_attn_x']
    _d['L0_attn_x'] = jax.random.normal(jax.random.fold_in(jax.random.key(seed), 1), (16, 512, 256), dtype=_x0.dtype)
    del _x0
    return _d

def reference(L0_attn_x, L0_attn_miu_x, L0_attn_lambda_, L0_attn_A_lora, L0_attn_B_lora, L0_attn_td_miu, L0_attn_td_A, L0_attn_td_B, L0_attn_u, L0_attn_Wr, L0_attn_Wk, L0_attn_Wv, L0_attn_Wg, L0_attn_Wo, L0_attn_gn_gamma, L0_attn_gn_beta, L0_ffn_gate_w, L0_ffn_fc1_w, L0_ffn_fc1_b, L0_ffn_geglu_mult, L0_ffn_fc2_w, L0_ffn_fc2_b, L0_ffn_s_fc1_w, L0_ffn_s_fc1_b, L0_ffn_s_geglu_mult, L0_ffn_s_fc2_w, L0_ffn_s_fc2_b):

    def _L0_attn_ref(x, miu_x, lambda_, A_lora, B_lora, td_miu, td_A, td_B, u, Wr, Wk, Wv, Wg, Wo, gn_gamma, gn_beta):
        import jax, jax.numpy as jnp
        import numpy as np
        B, T, C = (8, 512, 256)
        HS = 64
        H = C // HS
        LORA_R = 32
        TD_R = 64

        def _wkv6(r, k, v, w, u):
            n = r.shape[-1]
            decay = jnp.exp(-jnp.exp(w))

            def per_head(rt, kt, vt, dt, uh):

                def step(S, inp):
                    ri, ki, vi, di = inp
                    kv = ki[:, None] * vi[None, :]
                    y = ri @ (S + uh[:, None] * kv)
                    S = di[:, None] * S + kv
                    return (S, y)
                S0 = jnp.zeros((n, n), rt.dtype)
                _, ys = jax.lax.scan(step, S0, (rt, kt, vt, dt))
                return ys
            f = jax.vmap(per_head, in_axes=(0, 0, 0, 0, 0))
            f = jax.vmap(f, in_axes=(0, 0, 0, 0, None))
            return f(r, k, v, decay, u)
        b, t, c = x.shape
        h, n = u.shape
        x_last = jnp.pad(x, ((0, 0), (1, 0), (0, 0)))[:, :t]
        dxa = x_last - x
        xm = x + dxa * miu_x
        lora_h = jnp.tanh(xm @ A_lora).reshape(b, t, 5, -1)
        miu = lambda_ + jnp.einsum('btfi,fic->fbtc', lora_h, B_lora)
        xx = x[None] + dxa[None] * miu
        w_in, k_in, v_in, r_in, g_in = xx
        k = k_in @ Wk.T
        v = v_in @ Wv.T
        r = r_in @ Wr.T
        g = jax.nn.silu(g_in @ Wg.T)
        w = td_miu + jnp.tanh(w_in @ td_A) @ td_B

        def to_heads(z):
            return z.reshape(b, t, h, n).transpose(0, 2, 1, 3)
        y = _wkv6(to_heads(r), to_heads(k), to_heads(v), to_heads(w), u)
        y = y.transpose(0, 2, 1, 3)
        eps = 1e-05 * h
        mean = y.mean(-1, keepdims=True)
        var = y.var(-1, keepdims=True)
        yn = (y - mean) * jax.lax.rsqrt(var + eps)
        yn = yn * gn_gamma.reshape(h, n) + gn_beta.reshape(h, n)
        yn = yn.reshape(b, t, c)
        return yn * g @ Wo.T

    def _L0_ffn_ref(x, gate_w, fc1_w, fc1_b, geglu_mult, fc2_w, fc2_b, s_fc1_w, s_fc1_b, s_geglu_mult, s_fc2_w, s_fc2_b):
        import jax, jax.numpy as jnp
        import numpy as np
        S, B, D = (256, 2, 256)
        E, TOPK = (15, 3)
        F = 256
        FS = 512

        def _uinit(k, shape, out_dim):
            std = out_dim ** (-0.5)
            return jax.random.uniform(k, shape, jnp.float32, -std, std)
        s, b, d = x.shape
        xt = x.reshape(-1, d)
        T = xt.shape[0]
        logits = xt @ gate_w.T
        scores = jax.nn.softmax(logits, axis=-1)
        topk_w, topk_idx = jax.lax.top_k(scores, TOPK)
        topk_w = topk_w / (jnp.sum(topk_w, axis=-1, keepdims=True) + 1e-20)
        comb = jnp.zeros((T, E), xt.dtype).at[jnp.arange(T)[:, None], topk_idx].add(topk_w)
        h = jnp.einsum('td,efd->etf', xt, fc1_w) + fc1_b[:, None, :]
        xh, g = (h[..., :F], h[..., F:])
        a = jax.nn.gelu(g, approximate=False) * xh * geglu_mult[:, None, :]
        yexp = jnp.einsum('etf,edf->etd', a, fc2_w) + fc2_b[:, None, :]
        y = jnp.einsum('etd,te->td', yexp, comb)
        hs = xt @ s_fc1_w.T + s_fc1_b
        xs, gs = (hs[..., :FS], hs[..., FS:])
        as_ = jax.nn.gelu(gs, approximate=False) * xs * s_geglu_mult
        ys = as_ @ s_fc2_w.T + s_fc2_b
        return (y + ys).reshape(s, b, d)
    x = L0_attn_x
    x = _layernorm(x + _L0_attn_ref(x, L0_attn_miu_x, L0_attn_lambda_, L0_attn_A_lora, L0_attn_B_lora, L0_attn_td_miu, L0_attn_td_A, L0_attn_td_B, L0_attn_u, L0_attn_Wr, L0_attn_Wk, L0_attn_Wv, L0_attn_Wg, L0_attn_Wo, L0_attn_gn_gamma, L0_attn_gn_beta), axis=-1)
    x = _layernorm(x + _L0_ffn_ref(x, L0_ffn_gate_w, L0_ffn_fc1_w, L0_ffn_fc1_b, L0_ffn_geglu_mult, L0_ffn_fc2_w, L0_ffn_fc2_b, L0_ffn_s_fc1_w, L0_ffn_s_fc1_b, L0_ffn_s_geglu_mult, L0_ffn_s_fc2_w, L0_ffn_s_fc2_b), axis=-1)
    return x

_drawn_inputs = setup_inputs


def setup_inputs(seed=0):
    import zlib

    import numpy as np

    out = dict(_drawn_inputs(seed))
    spreads = {'L0_attn_gn_gamma': (1.0, 0.6),
     'L0_attn_gn_beta': (0.0, 0.8),
     'L0_ffn_geglu_mult': (1.0, 0.6),
     'L0_ffn_s_geglu_mult': (1.0, 0.6)}
    factors = {'L0_attn_miu_x': 8.0,
     'L0_attn_A_lora': 8.0,
     'L0_attn_B_lora': 8.0,
     'L0_attn_td_A': 64.0,
     'L0_attn_td_B': 64.0,
     'L0_attn_u': 38.899,
     'L0_ffn_fc1_b': 8.0,
     'L0_ffn_s_fc1_b': 8.0,
     'L0_attn_td_miu': 3.018}
    for name, (base, spread) in spreads.items():
        noise = np.random.default_rng([zlib.crc32(name.encode()), seed]).standard_normal(out[name].shape)
        drawn = base * np.exp(spread * noise) if base else spread * noise
        out[name] = jnp.asarray(drawn.astype(out[name].dtype))
    for name, factor in factors.items():
        out[name] = (out[name] * factor).astype(out[name].dtype)
    return out
```

```python
from contextlib import ExitStack

import numpy as np

import concourse.bass as bass
from concourse import mybir

ALU = mybir.AluOpType
ACT = mybir.ActivationFunctionType
F32 = mybir.dt.float32
BF16 = mybir.dt.bfloat16
I32 = mybir.dt.int32
U32 = mybir.dt.uint32
AX_X = mybir.AxisListType.X

P = 128
B, T, C = 16, 512, 256
HALVES = C // P
H, N = 4, 64
Q = T // P
CH = 64
NCH = T // CH
LORA = 32
TDR = 64
E, TOPK = 15, 3
F, FS = 256, 512
BUCKET = B * T
TILES = B * T * TOPK // P + E
SPARE = E
ROWS = E * BUCKET + (SPARE + E) * P
GN_EPS = 1e-5 * H
LN_EPS = 1e-5
MAGIC = 0x5F3759DF
NEWTON = 3

COLS = {}
_at = 0
for _name, _n in (("miu_x", 2), ("lambda", 10), ("td_miu", 2), ("u", 2), ("gamma", 2), ("beta", 2),
                  ("s_b1", 8), ("s_mult", 4), ("mult", 2 * E)):
    COLS[_name] = _at
    _at += _n
NCOLS = _at

ORDER = (
    ("lv", 0, 0), ("t", "N0", -1), ("p", "Mw", 1), ("lv", 1, 0), ("t", "N1", -1), ("p", "Mk", 1),
    ("lv", 2, 0), ("p", "TA", 1), ("t", "N2", -1), ("p", "Mv", 1), ("lv", 3, 0), ("p", "K", 1),
    ("t", "N3", -1), ("p", "TB", 1), ("t", "N4", -1), ("lv", 4, 0), ("t", "O0", -1), ("p", "Mr", 1),
    ("t", "O1", -1), ("lv", 5, 0), ("p", "V", 1), ("t", "R0", -1), ("p", "Mg", 1), ("t", "R1", -1),
    ("t", "R2", -1), ("t", "R3", -1), ("lv", 6, 0), ("p", "R", 1), ("t", "R4", -1), ("t", "R5", -1),
    ("p", "G", 1), ("y", 0, 0), ("p", "X", 2), ("y", 1, 0), ("t", "R6", -1), ("p", "L", 2),
    ("y", 2, 0), ("t", "R7", -1),
)
PJ = {"X": 0, "L": 2, "Mw": 4, "Mk": 6, "TA": 8, "Mv": 9, "K": 11, "TB": 13, "Mr": 15, "V": 17,
      "Mg": 19, "R": 21, "G": 23}
PJ_USES = 25
MIX = {"w": 0, "k": 1, "v": 2, "r": 3, "g": 4}
MIX_SLOT = {"w": 0, "k": 1, "v": 0, "r": 1, "g": 0}
MIX_RANK = {"w": 0, "k": 1, "v": 2, "r": 3, "g": 4}
MS = {"KT": 0, "Y": 2, "ZT": 4, "WO": 6, "XT": 8, "GATE": 10, "RANK": 11}
MS_USES = 12


def wait(eng, sem, value):
    if isinstance(value, int) and value <= 0:
        return
    eng.wait_ge(sem, value)


def ahead(eng, value):
    return value if isinstance(value, int) else eng.snap(value)


def wait_apart(eng, constants, *waits):
    waits = [(sem, value if isinstance(value, int) else eng.to_reg(value)) for sem, value in waits]
    eng.wait_ge(*constants)
    for sem, value in waits:
        wait(eng, sem, value)


def first(step):
    return isinstance(step, int) and step == 0


class Ring:

    def __init__(self, banks, full, free, uses):
        self.banks, self.full, self.free, self.uses = banks, full, free, uses

    def count(self, step, n):
        return step * len(range(n % 2, self.uses, 2)) + n // 2

    def bank(self, n):
        return self.banks[n % 2]

    def wait_full(self, eng, step, n):
        wait(eng, self.full[n % 2], self.count(step, n) + 1)

    def wait_free(self, eng, step, n):
        wait(eng, self.free[n % 2], self.count(step, n))

    def wait_read(self, eng, step, n):
        wait(eng, self.free[n % 2], self.count(step, n) + 1)


class Chain:

    def __init__(self, sem, per):
        self.sem, self.per, self.base, self.n = sem, per, 0, 0

    def start(self, step):
        self.base, self.n = step * self.per, 0

    def did(self, instruction):
        instruction.then_inc(self.sem, 1)
        self.n += 1

    def wait(self, eng):
        eng.wait_ge(self.sem, self.base + self.n)

    def wait_apart(self, eng, constants):
        wait_apart(eng, constants, (self.sem, self.base + self.n))

    def end(self):
        assert self.n == self.per, (self.n, self.per)


def rsqrt(dve, chain, y, v, half, t, var, scale, eps):
    chain.did(dve.tensor_scalar(v, var, scale, eps, ALU.mult, ALU.add))
    chain.wait(dve)
    chain.did(dve.tensor_scalar(half, v, -0.5, None, ALU.mult))
    chain.did(dve.tensor_scalar(t.bitcast(U32), v.bitcast(U32), 1, None, ALU.logical_shift_right))
    chain.wait(dve)
    chain.did(dve.tensor_scalar(y.bitcast(I32), t.bitcast(I32), -1.0, float(MAGIC), ALU.mult, ALU.add))
    for _ in range(NEWTON):
        chain.wait(dve)
        chain.did(dve.tensor_tensor(t, y, y, ALU.mult))
        chain.wait(dve)
        chain.did(dve.tensor_tensor(t, t, half, ALU.mult))
        chain.wait(dve)
        chain.did(dve.scalar_tensor_tensor(y, t, 1.5, y, ALU.add, ALU.mult))


RSQRT_STEPS = 4 + 3 * NEWTON


def build_program(nc, x, cols, rows, wk, wv, wr, wg, wo, a_lora, b_lora, td_a, td_b, gate, fc1, fc2,
                  s_fc1, s_fc2, out):
    x1_dram = nc.dram_tensor("x1_rows", (B * T, C), F32).ap()
    x1t_dram = nc.dram_tensor("x1_columns", (B, P, HALVES * T), F32).ap()
    bucket_in = nc.dram_tensor("bucket_in", (ROWS, C), F32).ap()
    tile_out = nc.dram_tensor("tile_out", (TILES * P, C), F32).ap()

    with ExitStack() as ctx:
        def sb(name, shape, dt=F32, stack=ctx):
            return stack.enter_context(nc.sbuf_tensor(name, shape, dt))

        def sem(name):
            return ctx.enter_context(nc.semaphore(name))

        vec = sb("vec", [P, NCOLS])
        ident = sb("ident", [P, P])
        weight = sb("weight", [P, B * Q, TOPK])
        slot = sb("slot", [P, B * Q, TOPK], U32)
        count = sb("count", [P, Q + 1, E])
        ebase = sb("ebase", [P, E])

        def column(name, n):
            return vec[:, COLS[name] + n:COLS[name] + n + 1]

        phase1(nc, sb, sem, column, vec, ident, weight, slot, count, ebase, x, cols, wk, wv, wr, wg, wo,
               a_lora, b_lora, td_a, td_b, gate, x1_dram, x1t_dram, bucket_in)
        phase2(nc, sb, sem, column, ident, slot, count, ebase, rows, fc1, fc2, bucket_in, tile_out)
        phase3(nc, sb, sem, column, weight, slot, rows, s_fc1, s_fc2, x1_dram, x1t_dram, tile_out, out)


def phase1(nc, sb_all, sem, column, vec, ident, weight, slot, count, ebase, x, cols, wk, wv, wr, wg, wo,
           a_lora, b_lora, td_a, td_b, gate, x1_dram, x1t_dram, bucket_in):
    with ExitStack() as ctx:
        def sb(name, shape, dt=F32):
            return sb_all(name, shape, dt, ctx)

        def ps(name, shape, dt=F32):
            return ctx.enter_context(nc.psum_tensor(name, shape, dt))

        w_k, w_v, w_r, w_g, w_o = (sb(f"w_{n}", [P, HALVES, C]) for n in "kvrgo")
        w_a = sb("w_a", [P, HALVES, 5 * LORA])
        w_b = sb("w_b", [P, C])
        w_b4 = sb("w_b4", [LORA, C])
        w_ta = sb("w_ta", [P, HALVES, TDR])
        w_tb = sb("w_tb", [TDR, C])
        w_gate = sb("w_gate", [P, HALVES, E])
        mask = sb("mask", [P, 7, CH], U32)
        half_gb = sb("half_gb", [P, 2 * HALVES])
        tri = sb("tri", [P, P], BF16)
        ones = sb("ones", [P, P], BF16)
        iota_e = sb("iota_e", [P, Q, E])
        iota_i = sb("iota_i", [P, Q * E], I32)
        ebase_i = sb("ebase_i", [P, E], I32)
        s_i, t_i, b_a, b_b, b_c, b_d = (sb(n, [P, CH], I32) for n in ("s_i", "t_i", "b_a", "b_b", "b_c", "b_d"))
        x_turn = sb("x_turn", [P, Q, C])
        xt = sb("xt", [P, HALVES, T + 1])
        dxa = sb("dxa", [P, HALVES, T])
        xm = sb("xm", [P, HALVES, T])
        lora = sb("lora", [P, T])
        lora4 = sb("lora4", [LORA, T])
        shifted = sb("shifted", [P, HALVES, T])
        mixed = sb("mixed", [P, 2, HALVES, T])
        tw = sb("tw", [TDR, T])
        ew = sb("ew", [P, HALVES, T])
        gate_t = sb("gate_t", [P, HALVES, T])
        k_, ku, r_, d_, g_ = ([sb(f"{n}{i}", [P, HALVES, T]) for i in range(2)] for n in ("k", "ku", "r", "d", "g"))
        v_ = [sb(f"v{i}", [P, Q, C]) for i in range(2)]
        dd = sb("dd", [P, HALVES, T])
        att = sb("att", [P, HALVES, 2, Q, CH])
        kt = sb("kt", [P, HALVES, Q, P])
        state = sb("state", [P, HALVES, NCH, N])
        yc = sb("yc", [P, Q, H, N])
        sq = sb("sq", [P, Q, H, N])
        stat = sb("stat", [P, 5, Q, H])
        zg = sb("zg", [P, HALVES, T])
        x_res = sb("x_res", [P, Q, C])
        res = sb("res", [P, Q, C])
        bn = sb("bn", [P, Q, 6])
        mv = sb("mv", [P, Q, 2])
        ln = sb("ln", [P, 5, Q])
        x1 = sb("x1", [P, Q, C])
        x1t = sb("x1t", [P, HALVES, T])
        logit = sb("logit", [P, Q, E + 1])
        prob = sb("prob", [P, Q, E + 1])
        rt = sb("rt", [P, 4, Q])
        top = sb("top", [P, Q, 8])
        top_i = sb("top_i", [P, Q, 8], U32)
        top_f = sb("top_f", [P, Q, 8])
        onehot = sb("onehot", [P, TOPK, Q * E])
        chosen = sb("chosen", [P, Q * E])
        chosen_b = sb("chosen_b", [P, Q * E], BF16)
        place = sb("place", [P, Q, E])
        picked = sb("picked", [P, TOPK, Q * E])
        slot_f = sb("slot_f", [P, Q, TOPK])
        slot_now = sb("slot_now", [P, Q, TOPK], U32)

        pj = Ring([ps(f"ps_pj{i}", [P, T]) for i in range(2)], [sem(f"pj_full{i}") for i in range(2)],
                  [sem(f"pj_free{i}") for i in range(2)], PJ_USES)
        ms = Ring([ps(f"ps_ms{i}", [P, T]) for i in range(2)], [sem(f"ms_full{i}") for i in range(2)],
                  [sem(f"ms_free{i}") for i in range(2)], MS_USES)
        lv = [[ps(f"ps_lv{i}{j}", [P, T]) for j in range(2)] for i in range(HALVES)]

        loaded = sem("loaded")
        made = sem("made")
        prep = sem("prep")
        xa_loaded = sem("xa_loaded")
        xr_loaded = sem("xr_loaded")
        dxa_done = sem("dxa_done")
        xm_ready = sem("xm_ready")
        mix_step = sem("mix_step")
        mixed_ready = sem("mixed_ready")
        ew_ready = sem("ew_ready")
        gate_ready = sem("gate_ready")
        mask_step = sem("mask_step")
        lv_full = [sem(f"lv_full{i}") for i in range(2)]
        lv_free = [sem(f"lv_free{i}") for i in range(2)]
        rkd = [sem(f"rkd{i}") for i in range(2)]
        state_step = [sem(f"state_step{i}") for i in range(2)]
        scored = sem("scored")
        norm_step = sem("norm_step")
        squared = sem("squared")
        yn_ready = sem("yn_ready")
        z_ready = sem("z_ready")
        ln_step = sem("ln_step")
        x1_ready = sem("x1_ready")
        x1_stored = sem("x1_stored")
        x1t_stored = sem("x1t_stored")
        route_step = sem("route_step")
        exp_ready = sem("exp_ready")
        chosen_ready = sem("chosen_ready")
        slots_ready = sem("slots_ready")
        scattered = sem("scattered")

        LOADS = 16 * 13
        MADE = 9
        PREP = 9
        NORM_STEPS = 3 * 2 + 1 + RSQRT_STEPS
        LN_STEPS = Q + Q + RSQRT_STEPS
        ROUTE_STEPS = 13 + 3 * TOPK + 3 * Q

        def doubled(hp, b, level):
            return rkd[hp], b * 18 + 3 * level

        def steps(eng, p_stage, lv_stage, y_stage, t_stage):
            stages = {"p": p_stage, "lv": lv_stage, "y": y_stage, "t": t_stage}

            def step(base, n):
                for kind, what, lead in ORDER:
                    if not isinstance(base, int) or 0 <= base + n + lead < B:
                        stages[kind](what, base + (n + lead), (n + lead) % 2)

            for n in range(-2, 2):
                step(0, n)
            with eng.Fori(0, (B - 4) // 2) as pair:
                for n in (2, 3):
                    step(pair * 2, n)
            for n in range(B - 2, B + 1):
                step(0, n)

        with nc.Block() as block:
            @block.sync
            def _(sp):
                for dst, src in ((vec[:], cols), (w_k[:], wk.rearrange("(h p) n -> p h n", p=P)),
                                 (w_v[:], wv.rearrange("(h p) n -> p h n", p=P)),
                                 (w_r[:], wr.rearrange("(h p) n -> p h n", p=P)),
                                 (w_g[:], wg.rearrange("(h p) n -> p h n", p=P)),
                                 (w_o[:], wo.rearrange("(h p) n -> p h n", p=P)),
                                 (w_b[:], b_lora[0:P, :]), (w_b4[:], b_lora[P:P + LORA, :]),
                                 (w_tb[:], td_b)):
                    sp.dma_start(dst, src).then_inc(loaded, 16)
                for dst, src in ((w_a[:], a_lora.rearrange("(h p) n -> p h n", p=P)),
                                 (w_ta[:], td_a.rearrange("(h p) n -> p h n", p=P)),
                                 (w_gate[:, 0, :], gate[0:P, :]), (w_gate[:, 1, :], gate[P:C, :])):
                    sp.dma_start(dst, src).then_inc(loaded, 16)

                def p_stage(what, b, par):
                    if what == "X":
                        at = ahead(sp, b * T)
                        if not first(b):
                            pj.wait_full(sp, b - 1, 1)
                        sp.dma_start(x_turn[:], x[bass.ds(at, T), :].rearrange("(q p) c -> p q c", p=P)
                                     ).then_inc(xa_loaded, 16)

                def lv_stage(level, b, par):
                    pass

                def y_stage(what, b, par):
                    pass

                def load_residual(at):
                    sp.dma_start(x_res[:], x[bass.ds(at, T), :].rearrange("(q p) c -> p q c", p=P)
                                 ).then_inc(xr_loaded, 16)

                def t_stage(what, b, par):
                    if what == "O1" and not (isinstance(b, int) and b == B - 1):
                        at = ahead(sp, b * T + T)
                        ms.wait_read(sp, b, MS["WO"] + 1)
                        load_residual(at)

                load_residual(0)
                steps(sp, p_stage, lv_stage, y_stage, t_stage)

            @block.gpsimd
            def _(pool):
                pool.iota(iota_i[:], pattern=[[0, Q], [1, E]], base=0, channel_multiplier=0).then_inc(made, 1)
                pool.iota(ebase_i[:], pattern=[[BUCKET, E]], base=0, channel_multiplier=0).then_inc(made, 1)
                pool.iota(s_i[:], pattern=[[0, CH]], base=0, channel_multiplier=1).then_inc(made, 1)
                pool.iota(t_i[:], pattern=[[1, CH]], base=0, channel_multiplier=0).then_inc(made, 1)
                pool.memset(ones[:], 1.0).then_inc(made, 1)
                pool.memset(tri[:], 1.0).then_inc(made, 1)
                pool.memset(ident[:], 0.0).then_inc(made, 1)
                pool.wait_ge(made, 7)
                pool.affine_select(out=ident[:], in_=ident[:], compare_op=ALU.not_equal, fill=1.0, base=0,
                                   pattern=[[-1, P]], channel_multiplier=1).then_inc(made, 1)
                pool.affine_select(out=tri[:], in_=tri[:], compare_op=ALU.is_gt, fill=0.0, base=0,
                                   pattern=[[1, P]], channel_multiplier=-1).then_inc(made, 1)

                def p_stage(what, b, par):
                    if what[0] != "M":
                        return
                    slot_of = MIX_SLOT[what[1]]
                    before = {"w": "G", "k": "R", "v": "TA", "r": "K", "g": "V"}[what[1]]
                    if what[1] in "vrg":
                        pj.wait_full(pool, b, PJ[before] + (before != "TA"))
                    elif not first(b):
                        pj.wait_full(pool, b - 1, PJ[before] + 1)
                    at = b * 10 + 2 * MIX_RANK[what[1]]
                    for hp in range(HALVES):
                        pj.wait_read(pool, b, PJ[what] + hp)
                        pool.tensor_tensor(mixed[:, slot_of, hp, :], shifted[:, hp, :], dxa[:, hp, :],
                                           ALU.mult).then_inc(mix_step, 1)
                    for hp in range(HALVES):
                        pool.wait_ge(mix_step, at + hp + 1)
                        pool.tensor_tensor(mixed[:, slot_of, hp, :], mixed[:, slot_of, hp, :], xt[:, hp, 1:T + 1],
                                           ALU.add).then_inc(mixed_ready, 1)

                def lv_stage(level, b, par):
                    pass

                def y_stage(what, b, par):
                    pass

                def t_stage(what, b, par):
                    if what == "R7":
                        wait_apart(pool, (made, MADE), (slots_ready, b + 1))
                        for q in range(Q):
                            for k in range(TOPK):
                                pool.indirect_dma_start(
                                    out=bucket_in, out_offset=bass.IndirectOffsetOnAxis(ap=slot_now[:, q, k:k + 1], axis=0),
                                    in_=x1[:, q, :], in_offset=None).then_inc(scattered, 16)

                steps(pool, p_stage, lv_stage, y_stage, t_stage)
                pool.wait_ge(scattered, 16 * B * Q * TOPK)

            @block.tensor
            def _(pe):
                pe.wait_ge(loaded, LOADS)
                pe.wait_ge(made, MADE)
                pe.wait_ge(prep, PREP)

                def p_stage(what, b, par):
                    n = PJ[what]
                    if what == "X":
                        pe.wait_ge(xa_loaded, 16 * (b + 1))
                        for hp in range(HALVES):
                            pj.wait_free(pe, b, n + hp)
                            for q in range(Q):
                                last = pe.transpose(pj.bank(n + hp)[:, q * P:(q + 1) * P],
                                                    x_turn[:, q, hp * P:(hp + 1) * P], ident[:])
                            last.then_inc(pj.full[(n + hp) % 2], 1)
                    elif what == "L":
                        pe.wait_ge(xm_ready, 2 * (b + 1))
                        for i, (rows_, first) in enumerate(((P, 0), (LORA, P))):
                            pj.wait_free(pe, b, n + i)
                            for hp in range(HALVES):
                                last = pe.matmul(pj.bank(n + i)[0:rows_, :], w_a[:, hp, first:first + rows_],
                                                 xm[:, hp, :], start=hp == 0, stop=hp == 1)
                            last.then_inc(pj.full[(n + i) % 2], 1)
                    elif what[0] == "M":
                        f = MIX[what[1]]
                        for hp in range(HALVES):
                            pj.wait_free(pe, b, n + hp)
                            wt, act_ = (w_b, lora) if f < 4 else (w_b4, lora4)
                            at = LORA * f if f < 4 else 0
                            last = pe.matmul(pj.bank(n + hp)[:], wt[at:at + LORA, hp * P:(hp + 1) * P],
                                             act_[at:at + LORA, :], start=True, stop=True)
                            last.then_inc(pj.full[(n + hp) % 2], 1)
                    elif what == "TA":
                        pe.wait_ge(mixed_ready, b * 10 + 2)
                        pj.wait_free(pe, b, n)
                        for hp in range(HALVES):
                            last = pe.matmul(pj.bank(n)[0:TDR, :], w_ta[:, hp, :], mixed[:, 0, hp, :],
                                             start=hp == 0, stop=hp == 1)
                        last.then_inc(pj.full[n % 2], 1)
                    elif what == "TB":
                        pj.wait_read(pe, b, PJ["TA"])
                        for hp in range(HALVES):
                            pj.wait_free(pe, b, n + hp)
                            last = pe.matmul(pj.bank(n + hp)[:], w_tb[:, hp * P:(hp + 1) * P], tw[:],
                                             start=True, stop=True)
                            last.then_inc(pj.full[(n + hp) % 2], 1)
                    elif what == "V":
                        pe.wait_ge(mixed_ready, b * 10 + 2 * MIX_RANK["v"] + 2)
                        for i in range(2):
                            pj.wait_free(pe, b, n + i)
                            for j in range(2):
                                q = 2 * i + j
                                for hp in range(HALVES):
                                    last = pe.matmul(pj.bank(n + i)[:, j * C:(j + 1) * C],
                                                     mixed[:, 0, hp, q * P:(q + 1) * P], w_v[:, hp, :],
                                                     start=hp == 0, stop=hp == 1)
                            last.then_inc(pj.full[(n + i) % 2], 1)
                    else:
                        f = what.lower()
                        w = {"k": w_k, "r": w_r, "g": w_g}[f]
                        pe.wait_ge(mixed_ready, b * 10 + 2 * MIX_RANK[f] + 2)
                        for hp in range(HALVES):
                            pj.wait_free(pe, b, n + hp)
                            for kk in range(HALVES):
                                last = pe.matmul(pj.bank(n + hp)[:], w[:, kk, hp * P:(hp + 1) * P],
                                                 mixed[:, MIX_SLOT[f], kk, :], start=kk == 0, stop=kk == 1)
                            last.then_inc(pj.full[(n + hp) % 2], 1)

                def lv_stage(level, b, par):
                    if level == 0:
                        for i in range(2):
                            pj.wait_read(pe, b, PJ["R"] + i)
                    left = ku[par] if level == 0 else k_[par]
                    for hp in range(HALVES):
                        ready = [doubled(hp, b, level - 1)] if level >= 2 else []
                        wait_apart(pe, (prep, PREP), (lv_free[hp], b * 8 + level), *ready)
                        for q in range(Q):
                            for h2, p2 in ((0, 0), (1, 1), (0, 1), (1, 0)):
                                t0 = (2 * q + p2) * CH
                                rows_ = slice(h2 * N, h2 * N + N)
                                last = pe.matmul(lv[hp][h2][p2 * CH:(p2 + 1) * CH, q * CH:(q + 1) * CH],
                                                 left[rows_, hp, t0:t0 + CH], r_[par][rows_, hp, t0:t0 + CH],
                                                 start=True, stop=True)
                        last.then_inc(lv_full[hp], 1)

                def y_stage(what, b, par):
                    if what == 0:
                        for hp in range(HALVES):
                            ms.wait_free(pe, b, hp)
                            pe.wait_ge(*doubled(hp, b, 6))
                            for q in range(Q):
                                last = pe.transpose(ms.bank(hp)[:, q * P:(q + 1) * P], k_[par][:, hp, q * P:(q + 1) * P],
                                                    ident[:])
                            last.then_inc(ms.full[hp], 1)
                    elif what == 1:
                        for i in range(2):
                            pj.wait_read(pe, b, PJ["V"] + i)
                        for hp in range(HALVES):
                            wait_apart(pe, (prep, PREP), (ms.free[hp], ms.count(b, hp) + 1), (lv_free[hp], b * 8 + 7))
                            for c in range(NCH - 1):
                                for h2 in range(2):
                                    p2 = c % 2
                                    rows_ = slice(p2 * CH, p2 * CH + CH)
                                    at = (2 * hp + h2) * N
                                    last = pe.matmul(lv[hp][p2][h2 * N:(h2 + 1) * N, c // 2 * N:(c // 2 + 1) * N],
                                                     kt[rows_, hp, c // 2, h2 * N:(h2 + 1) * N],
                                                     v_[par][rows_, c // 2, at:at + N], start=True, stop=True)
                            last.then_inc(lv_full[hp], 1)
                        n = MS["Y"]
                        for h2 in range(2):
                            for hp in range(HALVES):
                                for q in range(Q):
                                    for p2 in range(2):
                                        rows_ = slice(p2 * CH, (p2 + 1) * CH)
                                        h = 2 * hp + h2
                                        last = pe.matmul(ms.bank(n + h2)[rows_, (hp * Q + q) * N:(hp * Q + q + 1) * N],
                                                         att[rows_, hp, h2, q, :], v_[par][rows_, q, h * N:(h + 1) * N],
                                                         start=hp == 0 and q == 0, stop=False, skip_group_check=True)
                        last.then_inc(scored, 1)
                    else:
                        n = MS["Y"]
                        wait_apart(pe, (prep, PREP), (scored, b + 1), *((lv_free[hp], b * 8 + 8) for hp in range(HALVES)))
                        for hp in range(HALVES):
                            for q in range(Q):
                                for h2, p2 in ((0, 0), (1, 1), (0, 1), (1, 0)):
                                    c = 2 * q + p2
                                    rows_ = slice(h2 * N, h2 * N + N)
                                    last = pe.matmul(ms.bank(n + h2)[p2 * CH:(p2 + 1) * CH, (hp * Q + q) * N:(hp * Q + q + 1) * N],
                                                     r_[par][rows_, hp, c * CH:(c + 1) * CH], state[rows_, hp, c, :],
                                                     start=False, stop=hp == 1 and q == Q - 1, skip_group_check=True)
                                    if hp == 1 and q == Q - 1 and (h2, p2) in ((0, 1), (1, 0)):
                                        last.then_inc(ms.full[(n + h2) % 2], 1)

                def t_stage(what, b, par):
                    if what == "N3":
                        pe.wait_ge(yn_ready, b + 1)
                        for hp in range(HALVES):
                            n = MS["ZT"] + hp
                            ms.wait_free(pe, b, n)
                            for q in range(Q):
                                last = pe.transpose(ms.bank(n)[:, q * P:(q + 1) * P], yc[:, q, 2 * hp:2 * hp + 2, :], ident[:])
                            last.then_inc(ms.full[n % 2], 1)
                    elif what == "O0":
                        pe.wait_ge(z_ready, 2 * b + 2)
                        for i in range(2):
                            n = MS["WO"] + i
                            ms.wait_free(pe, b, n)
                            for j in range(2):
                                q = 2 * i + j
                                for hp in range(HALVES):
                                    last = pe.matmul(ms.bank(n)[:, j * C:(j + 1) * C], zg[:, hp, q * P:(q + 1) * P],
                                                     w_o[:, hp, :], start=hp == 0, stop=hp == 1)
                            last.then_inc(ms.full[n % 2], 1)
                    elif what == "R0":
                        pe.wait_ge(x1_ready, b + 1)
                        for hp in range(HALVES):
                            n = MS["XT"] + hp
                            ms.wait_free(pe, b, n)
                            for q in range(Q):
                                last = pe.transpose(ms.bank(n)[:, q * P:(q + 1) * P], x1[:, q, hp * P:(hp + 1) * P], ident[:])
                            last.then_inc(ms.full[n % 2], 1)
                    elif what == "R1":
                        n = MS["GATE"]
                        ms.wait_read(pe, b, MS["XT"] + 1)
                        ms.wait_free(pe, b, n)
                        for q in range(Q):
                            for hp in range(HALVES):
                                last = pe.matmul(ms.bank(n)[:, q * (E + 1):q * (E + 1) + E], x1t[:, hp, q * P:(q + 1) * P],
                                                 w_gate[:, hp, :], start=hp == 0, stop=hp == 1)
                        last.then_inc(ms.full[n % 2], 1)
                    elif what == "R4":
                        n = MS["RANK"]
                        pe.wait_ge(chosen_ready, b + 1)
                        ms.wait_free(pe, b, n)
                        pe.matmul(ms.bank(n)[:, 0:Q * E], tri[:], chosen_b[:], start=True, stop=True)
                        last = pe.matmul(ms.bank(n)[:, Q * E:2 * Q * E], ones[:], chosen_b[:], start=True, stop=True)
                        last.then_inc(ms.full[n % 2], 1)

                steps(pe, p_stage, lv_stage, y_stage, t_stage)

            @block.scalar
            def _(act):
                act.wait_ge(loaded, LOADS)
                act.wait_ge(prep, PREP)

                def p_stage(what, b, par):
                    n = PJ[what]

                    def read(i, instruction):
                        instruction.then_inc(pj.free[(n + i) % 2], 1)

                    if what == "X":
                        wait(act, mixed_ready, b * 10)
                        for hp in range(HALVES):
                            pj.wait_full(act, b, n + hp)
                            read(hp, act.activation(xt[:, hp, 1:T + 1], pj.bank(n + hp)[:], ACT.Copy))
                    elif what == "L":
                        for i, dst in enumerate((lora[:], lora4[:])):
                            pj.wait_full(act, b, n + i)
                            read(i, act.activation(dst, pj.bank(n + i)[0:dst.shape[0], :], ACT.Tanh))
                    elif what[0] == "M":
                        f = MIX[what[1]]
                        for hp in range(HALVES):
                            pj.wait_full(act, b, n + hp)
                            wait(act, mix_step, b * 10 + 2 * f + hp - 1)
                            read(hp, act.activation(shifted[:, hp, :], pj.bank(n + hp)[:], ACT.Identity,
                                                    bias=column("lambda", 2 * f + hp)))
                    elif what == "TA":
                        pj.wait_full(act, b, n)
                        read(0, act.activation(tw[:], pj.bank(n)[0:TDR, :], ACT.Tanh))
                    elif what == "TB":
                        if not (isinstance(b, int) and b < 2):
                            ms.wait_full(act, b - 2, MS["Y"] + 1)
                        for hp in range(HALVES):
                            pj.wait_full(act, b, n + hp)
                            act.activation(ew[:, hp, :], pj.bank(n + hp)[:], ACT.Exp, bias=column("td_miu", hp)
                                           ).then_inc(ew_ready, 1)
                            act.wait_ge(ew_ready, 2 * b + hp + 1)
                            read(hp, act.activation(d_[par][:, hp, :], ew[:, hp, :], ACT.Exp, scale=-1.0))
                    elif what == "K":
                        if not (isinstance(b, int) and b < 2):
                            for i in range(2):
                                ms.wait_full(act, b - 2, MS["Y"] + i)
                        for hp in range(HALVES):
                            pj.wait_full(act, b, n + hp)
                            act.activation(k_[par][:, hp, :], pj.bank(n + hp)[:], ACT.Copy)
                            read(hp, act.activation(ku[par][:, hp, :], pj.bank(n + hp)[:], ACT.Copy, scale=column("u", hp)))
                    elif what == "R":
                        for hp in range(HALVES):
                            pj.wait_full(act, b, n + hp)
                            read(hp, act.activation(r_[par][:, hp, :], pj.bank(n + hp)[:], ACT.Copy))
                    elif what == "V":
                        for i in range(2):
                            pj.wait_full(act, b, n + i)
                            read(i, act.activation(v_[par][:, 2 * i:2 * i + 2, :], pj.bank(n + i)[:].rearrange("p (q c) -> p q c", q=2),
                                                   ACT.Copy))
                    elif what == "G":
                        for hp in range(HALVES):
                            pj.wait_full(act, b, n + hp)
                            act.activation(gate_t[:, hp, :], pj.bank(n + hp)[:], ACT.Tanh, scale=0.5).then_inc(gate_ready, 1)

                def lv_stage(level, b, par):
                    pass

                def y_stage(what, b, par):
                    if what == 0:
                        for hp in range(HALVES):
                            ms.wait_full(act, b, hp)
                            act.activation(kt[:, hp, :, :], ms.bank(hp)[:].rearrange("p (q c) -> p q c", q=Q), ACT.Copy
                                           ).then_inc(ms.free[hp], 1)

                def t_stage(what, b, par):
                    if what in ("N0", "N1"):
                        h2 = int(what[1])
                        ms.wait_read(act, b, MS["Y"] + h2)
                        act.activation(sq[:, :, h2::2, :], yc[:, :, h2::2, :], ACT.Square).then_inc(squared, 1)
                    elif what == "N3":
                        for hp in range(HALVES):
                            n = MS["ZT"] + hp
                            ms.wait_full(act, b, n)
                            act.activation(zg[:, hp, :], ms.bank(n)[:], ACT.Identity, bias=half_gb[:, 2 + hp:3 + hp],
                                           scale=half_gb[:, hp:hp + 1]).then_inc(ms.free[n % 2], 1)
                    elif what == "R0":
                        wait(act, x1t_stored, 16 * b)
                        for hp in range(HALVES):
                            n = MS["XT"] + hp
                            ms.wait_full(act, b, n)
                            act.activation(x1t[:, hp, :], ms.bank(n)[:], ACT.Copy).then_inc(ms.free[n % 2], 1)
                        act.wait_ge(x1_ready, b + 1)
                        act.dma_start(x1_dram[bass.ds(b * T, T), :].rearrange("(q p) c -> p q c", p=P), x1[:]
                                      ).then_inc(x1_stored, 16)
                        for hp in range(HALVES):
                            ms.wait_read(act, b, MS["XT"] + hp)
                        act.dma_start(x1t_dram[bass.ds(b, 1), :, :].rearrange("o p c -> (o p) c"),
                                      x1t[:].rearrange("p h t -> p (h t)")).then_inc(x1t_stored, 16)
                    elif what == "R2":
                        ms.wait_read(act, b, MS["GATE"])
                        act.activation(prob[:, :, 0:E], logit[:, :, 0:E], ACT.Exp).then_inc(exp_ready, 1)

                steps(act, p_stage, lv_stage, y_stage, t_stage)
                act.wait_ge(x1_stored, 16 * B)
                act.wait_ge(x1t_stored, 16 * B)

            @block.vector
            def _(dve):
                norm, lnc, route = Chain(norm_step, NORM_STEPS), Chain(ln_step, LN_STEPS), Chain(route_step, ROUTE_STEPS)
                dve.memset(xt[:, :, 0:1], 0.0).then_inc(prep, 1)
                dve.memset(att[:], 0.0).then_inc(prep, 1)
                dve.memset(count[:], 0.0).then_inc(prep, 1)
                dve.memset(state[:, :, 0, :], 0.0).then_inc(prep, 1)
                dve.wait_ge(loaded, LOADS)
                dve.tensor_scalar(half_gb[:], vec[:, COLS["gamma"]:COLS["gamma"] + 4], 0.5, None, ALU.mult).then_inc(prep, 1)
                dve.wait_ge(made, MADE)
                dve.tensor_copy(iota_e[:].rearrange("p q e -> p (q e)"), iota_i[:]).then_inc(prep, 1)
                dve.tensor_copy(ebase[:], ebase_i[:]).then_inc(prep, 1)
                dve.tensor_scalar(s_i[:], s_i[:], CH - 1, None, ALU.bitwise_and).then_inc(prep, 1)
                dve.wait_ge(prep, 8)
                dve.tensor_tensor(mask[:, 0, :], s_i[:], t_i[:], ALU.is_equal).then_inc(prep, 1)
                mk = 0
                for level in range(1, 7):
                    m = 1 << (level - 1)
                    dve.tensor_scalar(b_a[:], s_i[:], 2 * m - 1, None, ALU.bitwise_or).then_inc(mask_step, 1)
                    dve.tensor_scalar(b_b[:], t_i[:], 2 * m - 1, None, ALU.bitwise_or).then_inc(mask_step, 1)
                    dve.tensor_scalar(b_c[:], s_i[:], m, None, ALU.bitwise_and).then_inc(mask_step, 1)
                    dve.tensor_scalar(b_d[:], t_i[:], m, None, ALU.bitwise_and).then_inc(mask_step, 1)
                    dve.wait_ge(mask_step, mk + 4)
                    dve.tensor_tensor(b_a[:], b_a[:], b_b[:], ALU.is_equal).then_inc(mask_step, 1)
                    dve.tensor_tensor(b_c[:], b_d[:], b_c[:], ALU.is_gt).then_inc(mask_step, 1)
                    dve.wait_ge(mask_step, mk + 6)
                    dve.tensor_tensor(mask[:, level, :], b_a[:], b_c[:], ALU.mult).then_inc(mask_step, 1)
                    mk += 7
                    dve.wait_ge(mask_step, mk)
                dve.wait_ge(prep, PREP)

                def p_stage(what, b, par):
                    if what == "X":
                        for hp in range(HALVES):
                            pj.wait_read(dve, b, PJ["X"] + hp)
                        dve.tensor_tensor(dxa[:], xt[:, :, 0:T], xt[:, :, 1:T + 1], ALU.subtract).then_inc(dxa_done, 1)
                        dve.wait_ge(dxa_done, b + 1)
                        for hp in range(HALVES):
                            if not first(b):
                                pj.wait_full(dve, b - 1, PJ["L"] + 1)
                            dve.scalar_tensor_tensor(xm[:, hp, :], dxa[:, hp, :], column("miu_x", hp), xt[:, hp, 1:T + 1],
                                                     ALU.mult, ALU.add).then_inc(xm_ready, 1)
                    elif what == "G":
                        n = PJ[what]
                        wait(dve, z_ready, 2 * (b - 1)) if not (isinstance(b, int) and b < 2) else None
                        for hp in range(HALVES):
                            dve.wait_ge(gate_ready, 2 * b + hp + 1)
                            dve.scalar_tensor_tensor(g_[par][:, hp, :], gate_t[:, hp, :], 1.0, pj.bank(n + hp)[:], ALU.add,
                                                     ALU.mult).then_inc(pj.free[(n + hp) % 2], 1)

                def lv_stage(level, b, par):
                    if level == 0:
                        for hp in range(HALVES):
                            pj.wait_read(dve, b, PJ["R"] + hp)
                    for hp in range(HALVES):
                        wait_apart(dve, (prep, PREP), (lv_full[hp], b * 8 + level + 1))
                        for h2 in range(2):
                            ins = dve.copy_predicated(att[:, hp, h2, :, :], mask[:, level, :].unsqueeze(1).to_broadcast([P, Q, CH]),
                                                      lv[hp][h2][:, 0:Q * CH].rearrange("p (q t) -> p q t", t=CH))
                        ins.then_inc(lv_free[hp], 1)
                        if level:
                            m = 1 << (level - 1)
                            nb = T // (2 * m)
                            if level == 1:
                                d_in = d_[par][:, hp, :]
                            else:
                                at = T - (T >> (level - 2))
                                d_in = dd[:, hp, at:at + T // m]
                                dve.wait_ge(*doubled(hp, b, level - 1))
                            d_in = d_in.rearrange("p (n two) -> p n two", two=2)
                            at = T - (T >> (level - 1))
                            dve.tensor_tensor(dd[:, hp, at:at + nb], d_in[:, :, 0], d_in[:, :, 1], ALU.mult).then_inc(rkd[hp], 1)
                            rv = r_[par][:, hp, :].rearrange("p (n two m) -> p n two m", two=2, m=m)[:, :, 1, :]
                            kv = k_[par][:, hp, :].rearrange("p (n two m) -> p n two m", two=2, m=m)[:, :, 0, :]
                            dve.tensor_tensor(rv, rv, d_in[:, :, 0].unsqueeze(2).to_broadcast([P, nb, m]), ALU.mult
                                              ).then_inc(rkd[hp], 1)
                            dve.tensor_tensor(kv, kv, d_in[:, :, 1].unsqueeze(2).to_broadcast([P, nb, m]), ALU.mult
                                              ).then_inc(rkd[hp], 1)

                def y_stage(what, b, par):
                    if what == 1:
                        for c in range(NCH - 1):
                            for hp in range(HALVES):
                                if c == 0:
                                    dve.wait_ge(lv_full[hp], b * 8 + 8)
                                    ins = dve.tensor_copy(state[:, hp, 1, :], lv[hp][0][:, 0:N])
                                else:
                                    at = T - (T >> 5) + c
                                    if c == 1:
                                        dve.wait_ge(*doubled(hp, b, 6))
                                    dve.wait_ge(state_step[hp], b * 6 + c)
                                    ins = dve.scalar_tensor_tensor(state[:, hp, c + 1, :], state[:, hp, c, :],
                                                                   dd[:, hp, at:at + 1], lv[hp][c % 2][:, c // 2 * N:(c // 2 + 1) * N],
                                                                   ALU.mult, ALU.add)
                                ins.then_inc(lv_free[hp] if c == NCH - 2 else state_step[hp], 1)

                def did(ins):
                    route.did(ins)
                    route.wait_apart(dve, (prep, PREP))

                def t_stage(what, b, par):
                    if what in ("N0", "N1"):
                        h2 = int(what[1])
                        if h2 == 0:
                            norm.start(b)
                        ms.wait_full(dve, b, MS["Y"] + h2)
                        for hp in range(HALVES):
                            yv = ms.bank(h2)[:, hp * Q * N:(hp + 1) * Q * N].rearrange("p (q n) -> p q n", n=N)
                            norm.did(dve.tensor_reduce(stat[:, 0, :, 2 * hp + h2], yv, AX_X, ALU.add))
                        norm.wait(dve)
                        norm.did(dve.tensor_scalar(stat[:, 0, :, h2::2], stat[:, 0, :, h2::2], 1.0 / N, None, ALU.mult))
                        norm.wait(dve)
                        for hp in range(HALVES):
                            yv = ms.bank(h2)[:, hp * Q * N:(hp + 1) * Q * N].rearrange("p (q n) -> p q n", n=N)
                            ins = dve.tensor_tensor(yc[:, :, 2 * hp + h2, :], yv,
                                                    stat[:, 0, :, 2 * hp + h2].unsqueeze(2).to_broadcast([P, Q, N]), ALU.subtract)
                        ins.then_inc(ms.free[h2], 1)
                    elif what == "N2":
                        dve.wait_ge(squared, 2 * b + 2)
                        norm.did(dve.tensor_reduce(stat[:, 1, :, :], sq[:], AX_X, ALU.add))
                        norm.wait(dve)
                        rsqrt(dve, norm, *(stat[:, i, :, :].rearrange("p q h -> p (q h)") for i in (0, 2, 3, 4, 1)),
                              1.0 / N, GN_EPS)
                        norm.wait(dve)
                        norm.end()
                        ycv = yc[:].rearrange("p q h n -> p (q h) n")
                        dve.tensor_tensor(ycv, ycv, stat[:, 0, :, :].rearrange("p q h -> p (q h)").unsqueeze(2).to_broadcast([P, Q * H, N]), ALU.mult
                                          ).then_inc(yn_ready, 1)
                    elif what == "N4":
                        for hp in range(HALVES):
                            ms.wait_read(dve, b, MS["ZT"] + hp)
                            dve.tensor_tensor(zg[:, hp, :], zg[:, hp, :], g_[par][:, hp, :], ALU.mult).then_inc(z_ready, 1)
                    elif what == "O1":
                        lnc.start(b)
                        dve.wait_ge(xr_loaded, 16 * (b + 1))
                        for i in range(2):
                            n = MS["WO"] + i
                            ms.wait_full(dve, b, n)
                            dve.tensor_tensor(res[:, 2 * i:2 * i + 2, :], ms.bank(n)[:].rearrange("p (q c) -> p q c", q=2),
                                              x_res[:, 2 * i:2 * i + 2, :], ALU.add).then_inc(ms.free[n % 2], 1)
                        for i in range(2):
                            ms.wait_read(dve, b, MS["WO"] + i)
                        for q in range(Q):
                            lnc.did(dve.bn_stats(bn[:, q, :], res[:, q, :]))
                        for q in range(Q):
                            if q == 0:
                                lnc.wait_apart(dve, (prep, PREP))
                            lnc.did(dve.bn_aggr(mv[:, q, :], bn[:, q, :]))
                        lnc.wait(dve)
                        rsqrt(dve, lnc, ln[:, 0, :], ln[:, 1, :], ln[:, 2, :], ln[:, 3, :], mv[:, :, 1], 1.0, LN_EPS)
                        lnc.wait(dve)
                        lnc.end()
                        wait(dve, x1_stored, 16 * b)
                        wait(dve, scattered, 16 * Q * TOPK * b)
                        for q in range(Q):
                            ins = dve.tensor_scalar(x1[:, q, :], res[:, q, :], mv[:, q, 0:1], ln[:, 0, q:q + 1],
                                                    ALU.subtract, ALU.mult)
                        ins.then_inc(x1_ready, 1)
                    elif what == "R2":
                        route.start(b)
                        n = MS["GATE"]
                        ms.wait_full(dve, b, n)
                        gates = ms.bank(n)[:, 0:Q * (E + 1)].rearrange("p (q e) -> p q e", q=Q)[:, :, 0:E]
                        did(dve.tensor_reduce(rt[:, 0, :], gates, AX_X, ALU.max))
                        dve.tensor_tensor(logit[:, :, 0:E], gates, rt[:, 0, :].unsqueeze(2).to_broadcast([P, Q, E]),
                                          ALU.subtract).then_inc(ms.free[n % 2], 1)
                    elif what == "R3":
                        dve.wait_ge(exp_ready, b + 1)
                        did(dve.tensor_reduce(rt[:, 1, :], prob[:, :, 0:E], AX_X, ALU.add))
                        did(dve.reciprocal(rt[:, 2, :], rt[:, 1, :]))
                        did(dve.tensor_tensor(prob[:, :, 0:E], prob[:, :, 0:E],
                                              rt[:, 2, :].unsqueeze(2).to_broadcast([P, Q, E]), ALU.mult))
                        for q in range(Q):
                            route.did(dve.max(top[:, q, :], prob[:, q, 0:E]))
                        route.wait_apart(dve, (prep, PREP))
                        for q in range(Q):
                            route.did(dve.max_index(top_i[:, q, :], top[:, q, :], prob[:, q, 0:E]))
                        did(dve.tensor_reduce(rt[:, 1, :], top[:, :, 0:TOPK], AX_X, ALU.add))
                        did(dve.tensor_scalar(rt[:, 1, :], rt[:, 1, :], 1e-20, None, ALU.add))
                        did(dve.reciprocal(rt[:, 2, :], rt[:, 1, :]))
                        did(dve.tensor_tensor(weight[:, bass.ds(b * Q, Q), :], top[:, :, 0:TOPK],
                                              rt[:, 2, :].unsqueeze(2).to_broadcast([P, Q, TOPK]), ALU.mult))
                        did(dve.tensor_copy(top_f[:], top_i[:]))
                        for k in range(TOPK):
                            route.did(dve.tensor_tensor(onehot[:, k, :].rearrange("p (q e) -> p q e", q=Q), iota_e[:],
                                                        top_f[:, :, k:k + 1].to_broadcast([P, Q, E]), ALU.is_equal))
                        route.wait(dve)
                        did(dve.tensor_tensor(chosen[:], onehot[:, 0, :], onehot[:, 1, :], ALU.add))
                        dve.tensor_tensor(chosen_b[:], chosen[:], onehot[:, 2, :], ALU.add).then_inc(chosen_ready, 1)
                    elif what == "R5":
                        n = MS["RANK"]
                        ms.wait_full(dve, b, n)
                        sums = ms.bank(n)[:, Q * E:2 * Q * E].rearrange("p (q e) -> p q e", q=Q)
                        for q in range(Q):
                            did(dve.tensor_tensor(count[:, q + 1, :], count[:, q, :], sums[:, q, :], ALU.add))
                        dve.tensor_tensor(place[:], ms.bank(n)[:, 0:Q * E].rearrange("p (q e) -> p q e", q=Q),
                                          count[:, 0:Q, :], ALU.add).then_inc(ms.free[n % 2], 1)
                    elif what == "R6":
                        ms.wait_read(dve, b, MS["RANK"])
                        did(dve.tensor_tensor(place[:], place[:], ebase[:].unsqueeze(1).to_broadcast([P, Q, E]), ALU.add))
                        for k in range(TOPK):
                            route.did(dve.tensor_tensor(picked[:, k, :], onehot[:, k, :], place[:].rearrange("p q e -> p (q e)"),
                                                        ALU.mult))
                        did(dve.tensor_copy(count[:, 0, :], count[:, Q, :]))
                        for k in range(TOPK):
                            route.did(dve.tensor_reduce(slot_f[:, :, k], picked[:, k, :].rearrange("p (q e) -> p q e", q=Q),
                                                        AX_X, ALU.add))
                        route.wait(dve)
                        did(dve.tensor_copy(slot[:, bass.ds(b * Q, Q), :], slot_f[:]))
                        wait(dve, scattered, 16 * Q * TOPK * b)
                        dve.tensor_copy(slot_now[:], slot_f[:]).then_inc(slots_ready, 1)
                        route.end()

                steps(dve, p_stage, lv_stage, y_stage, t_stage)


def phase2(nc, sb_all, sem, column, ident, slot, count, ebase, rows, fc1, fc2, bucket_in, tile_out):
    with ExitStack() as ctx:
        def sb(name, shape, dt=F32):
            return sb_all(name, shape, dt, ctx)

        def ps(name, shape, dt=F32):
            return ctx.enter_context(nc.psum_tensor(name, shape, dt))

        w1 = sb("w1", [P, E, HALVES * 2 * F])
        w2 = sb("w2", [P, E, HALVES * C])
        b1 = sb("b1", [P, E, 2 * F])
        b2 = sb("b2", [P, E, C])
        zeros = sb("zeros", [P, C])
        number = sb("number", [P, TILES], I32)
        number_f = sb("number_f", [P, TILES])
        row_i = sb("row_i", [P, E], I32)
        row_f = sb("row_f", [P, E])
        spare_i = sb("spare_i", [P, E], I32)
        spare_f = sb("spare_f", [P, E])
        tiles_i = sb("tiles_i", [P, E], I32)
        tiles = sb("tiles", [P, E])
        ends = sb("ends", [P, E])
        one_e = sb("one_e", [P, E])
        past = sb("past", [P, TILES])
        past_t = sb("past_t", [P, TILES])
        before = sb("before", [P, TILES])
        sched_e = sb("sched_e", [P, TILES], I32)
        sched_r = sb("sched_r", [P, TILES], I32)
        sched_f = sb("sched_f", [P, TILES])
        pad_f = sb("pad_f", [P, E])
        slot_e = sb("slot_e", [P, B * Q * TOPK], U32)
        slot_ef = sb("slot_ef", [P, B * Q * TOPK])
        slot_f = sb("slot_all_f", [P, B * Q * TOPK])
        slot_d = sb("slot_d", [P, B * Q * TOPK])
        delta = sb("delta", [P, E])
        pad_m = sb("pad_m", [P, E])
        pad_row = sb("pad_row", [P, E], U32)
        rows_in = [sb(f"rows_in{i}", [P, C]) for i in range(2)]
        rows_t = [sb(f"rows_t{i}", [P, HALVES, P]) for i in range(2)]
        hidden = [sb(f"hidden{i}", [P, 2 * F]) for i in range(2)]
        gelu = [sb(f"gelu{i}", [P, F]) for i in range(2)]
        acts = [sb(f"acts{i}", [P, F]) for i in range(2)]
        acts_t = [sb(f"acts_t{i}", [P, HALVES, P]) for i in range(2)]
        rows_out = [sb(f"rows_out{i}", [P, C]) for i in range(2)]
        xt_ps = [ps(f"ps_xt{i}", [P, T]) for i in range(2)]
        h_ps = [ps(f"ps_h{i}", [P, T]) for i in range(2)]
        at_ps = [ps(f"ps_at{i}", [P, T]) for i in range(2)]
        o_ps = [ps(f"ps_o{i}", [P, T]) for i in range(2)]

        weights_loaded = sem("weights_loaded")
        numbers_made = sem("numbers_made")
        zeros_made = sem("zeros_made")
        plan = sem("plan")
        planned = sem("planned")
        pads_ready = sem("pads_ready")
        padded = sem("padded")
        scaled = sem("scaled")
        rows_loaded = [sem(f"rows_loaded{i}") for i in range(2)]
        rows_stored = [sem(f"rows_stored{i}") for i in range(2)]
        turned = sem("turned")
        rows_t_ready = sem("rows_t_ready")
        first_done = sem("first_done")
        hidden_ready = sem("hidden_ready")
        gelu_ready = sem("gelu_ready")
        acts_ready = sem("acts_ready")
        acts_turned = sem("acts_turned")
        acts_t_ready = sem("acts_t_ready")
        second_done = sem("second_done")
        out_ready = sem("out_ready")
        DUMMY = E * BUCKET

        LEAD = {"A": 2, "B": 1, "C": 0, "D": -1}

        def steps(stage, order):
            def one(i, par, has):
                for name in order:
                    if has(name, LEAD[name]):
                        stage(name, i + LEAD[name], (par + LEAD[name]) % 2)

            def valid(i):
                return lambda name, ahead: 0 <= i + ahead < TILES
            for i in range(-2, 3):
                one(i, i % 2, valid(i))
            loops = (TILES - 5) // 2
            yield loops, one
            for i in range(3 + 2 * loops, TILES + 1):
                one(i, i % 2, valid(i))

        def run(eng, stage, order):
            for loops, one in steps(stage, order):
                with eng.Fori(0, loops) as n:
                    for half in range(2):
                        one(n * 2 + (3 + half), 1 - half, lambda name, ahead: True)

        def turn(tile, par):
            return (tile - par) // 2 if isinstance(tile, int) else (tile - par) // 2

        with nc.Block() as block:
            @block.sync
            def _(sp):
                for kk in range(HALVES):
                    sp.dma_start(w1[:, :, kk * 2 * F:(kk + 1) * 2 * F],
                                 fc1[:, kk * P:(kk + 1) * P, :].rearrange("e p f -> p e f")).then_inc(weights_loaded, 16)
                    sp.dma_start(w2[:, :, kk * C:(kk + 1) * C],
                                 fc2[:, kk * P:(kk + 1) * P, :].rearrange("e p f -> p e f")).then_inc(weights_loaded, 16)
                sp.dma_start(b1[:].rearrange("p e f -> p (e f)"),
                             rows[0:1, 0:E * 2 * F].partition_broadcast(P).rearrange("p o n -> p (o n)")).then_inc(weights_loaded, 16)
                sp.dma_start(b2[:].rearrange("p e f -> p (e f)"),
                             rows[0:1, E * 2 * F:E * 2 * F + E * C].partition_broadcast(P).rearrange("p o n -> p (o n)")
                             ).then_inc(weights_loaded, 16)
                sp.wait_ge(planned, 1)
                sp.wait_ge(padded, 16 * (E + 1))

                def stage(name, tile, par):
                    if name == "A":
                        row = sp.value_load(sched_r[0:1, bass.ds(tile, 1)], min_val=0, max_val=ROWS - P)
                        if not isinstance(tile, int) or tile >= 2:
                            sp.wait_ge(turned, tile - 1)
                        sp.dma_start(rows_in[par][:], bucket_in[bass.ds(row, P), :]).then_inc(rows_loaded[par], 16)

                run(sp, stage, "A")

            @block.gpsimd
            def _(pool):
                pool.memset(zeros[:], 0.0).then_inc(zeros_made, 1)
                pool.iota(number[:], pattern=[[1, TILES]], base=0, channel_multiplier=0).then_inc(numbers_made, 1)
                pool.iota(row_i[:], pattern=[[0, E]], base=0, channel_multiplier=1).then_inc(numbers_made, 1)
                pool.iota(spare_i[:], pattern=[[P, E]], base=DUMMY + SPARE * P, channel_multiplier=1
                          ).then_inc(numbers_made, 1)
                pool.wait_ge(zeros_made, 1)
                pool.dma_start(bucket_in[DUMMY:DUMMY + SPARE * P, :].rearrange("(s p) c -> p s c", p=P),
                               zeros[:].unsqueeze(1).to_broadcast([P, SPARE, C])).then_inc(padded, 16)
                pool.wait_ge(pads_ready, 1)
                for e in range(E):
                    pool.indirect_dma_start(out=bucket_in, out_offset=bass.IndirectOffsetOnAxis(ap=pad_row[:, e:e + 1], axis=0),
                                            in_=zeros[:], in_offset=None).then_inc(padded, 16)

            @block.tensor
            def _(pe):
                pe.wait_ge(planned, 1)
                pe.wait_ge(weights_loaded, 16 * 6)
                pe.wait_ge(scaled, HALVES * E)

                def stage(name, tile, par):
                    if name == "A":
                        pe.wait_ge(rows_loaded[par], 16 * (turn(tile, par) + 1))
                        if not isinstance(tile, int) or tile >= 2:
                            pe.wait_ge(rows_t_ready, tile - 1)
                        for kk in range(HALVES):
                            last = pe.transpose(xt_ps[par][:, kk * P:(kk + 1) * P], rows_in[par][:, kk * P:(kk + 1) * P], ident[:])
                        last.then_inc(turned, 1)
                    elif name == "B":
                        e = pe.value_load(sched_e[0:1, bass.ds(tile, 1)], min_val=0, max_val=E - 1)
                        pe.wait_ge(rows_t_ready, tile + 1)
                        if not isinstance(tile, int) or tile >= 2:
                            pe.wait_ge(hidden_ready, tile - 1)
                        for kk in range(HALVES):
                            last = pe.matmul(h_ps[par][:], rows_t[par][:, kk, :],
                                             w1[:, bass.ds(e, 1), kk * 2 * F:(kk + 1) * 2 * F].rearrange("p o f -> p (o f)"),
                                             start=kk == 0, stop=kk == 1)
                        last.then_inc(first_done, 1)
                    elif name == "C":
                        pe.wait_ge(acts_ready, tile + 1)
                        if not isinstance(tile, int) or tile >= 2:
                            pe.wait_ge(acts_t_ready, tile - 1)
                        for kk in range(HALVES):
                            last = pe.transpose(at_ps[par][:, kk * P:(kk + 1) * P], acts[par][:, kk * P:(kk + 1) * P], ident[:])
                        last.then_inc(acts_turned, 1)
                    else:
                        e = pe.value_load(sched_e[0:1, bass.ds(tile, 1)], min_val=0, max_val=E - 1)
                        pe.wait_ge(acts_t_ready, tile + 1)
                        if not isinstance(tile, int) or tile >= 2:
                            pe.wait_ge(out_ready, tile - 1)
                        for kk in range(HALVES):
                            last = pe.matmul(o_ps[par][:, 0:C], acts_t[par][:, kk, :],
                                             w2[:, bass.ds(e, 1), kk * C:(kk + 1) * C].rearrange("p o f -> p (o f)"),
                                             start=kk == 0, stop=kk == 1)
                        last.then_inc(second_done, 1)

                run(pe, stage, "BACD")

            @block.scalar
            def _(act):
                def stage(name, tile, par):
                    if name == "A":
                        act.wait_ge(turned, tile + 1)
                        if not isinstance(tile, int) or tile >= 2:
                            act.wait_ge(first_done, tile - 1)
                        act.activation(rows_t[par][:], xt_ps[par][:, 0:C].rearrange("p (k t) -> p k t", k=HALVES), ACT.Copy
                                       ).then_inc(rows_t_ready, 1)
                    elif name == "B":
                        act.wait_ge(hidden_ready, tile + 1)
                        if not isinstance(tile, int) or tile >= 2:
                            act.wait_ge(acts_ready, tile - 1)
                        act.activation(gelu[par][:], hidden[par][:, F:2 * F], ACT.Gelu).then_inc(gelu_ready, 1)
                    elif name == "C":
                        act.wait_ge(acts_turned, tile + 1)
                        if not isinstance(tile, int) or tile >= 2:
                            act.wait_ge(second_done, tile - 1)
                        act.activation(acts_t[par][:], at_ps[par][:, 0:F].rearrange("p (k t) -> p k t", k=HALVES), ACT.Copy
                                       ).then_inc(acts_t_ready, 1)
                    else:
                        row = ahead(act, tile * P)
                        act.wait_ge(out_ready, tile + 1)
                        act.dma_start(tile_out[bass.ds(row, P), :], rows_out[par][:]).then_inc(rows_stored[par], 16)

                act.wait_ge(planned, 1)
                run(act, stage, "ACBD")
                act.wait_ge(rows_stored[0], 16 * ((TILES + 1) // 2))
                act.wait_ge(rows_stored[1], 16 * (TILES // 2))

            @block.vector
            def _(dve):
                n = 0

                def did(ins):
                    nonlocal n
                    ins.then_inc(plan, 1)
                    n += 1
                    dve.wait_ge(plan, n)

                dve.wait_ge(numbers_made, 3)
                total = count[:, 0, :]
                did(dve.tensor_scalar(tiles[:], total, float(P - 1), None, ALU.add))
                did(dve.tensor_copy(tiles_i[:], tiles[:]))
                did(dve.tensor_scalar(tiles_i[:], tiles_i[:], 7, None, ALU.arith_shift_right))
                did(dve.tensor_copy(tiles[:], tiles_i[:]))
                did(dve.memset(one_e[:], 1.0))
                did(dve.tensor_tensor_scan(ends[:], one_e[:], tiles[:], 0.0, ALU.mult, ALU.add))
                did(dve.tensor_copy(number_f[:], number[:]))
                did(dve.tensor_copy(row_f[:], row_i[:]))
                did(dve.tensor_tensor(pad_f[:], row_f[:], total, ALU.add))
                did(dve.tensor_scalar(pad_m[:], tiles[:], float(P), None, ALU.mult))
                did(dve.tensor_tensor(pad_m[:], pad_f[:], pad_m[:], ALU.is_lt))
                did(dve.tensor_tensor(pad_f[:], pad_f[:], ebase[:], ALU.add))
                did(dve.tensor_copy(spare_f[:], spare_i[:]))
                did(dve.tensor_tensor(pad_f[:], pad_f[:], spare_f[:], ALU.subtract))
                did(dve.tensor_tensor(pad_f[:], pad_f[:], pad_m[:], ALU.mult))
                did(dve.tensor_tensor(pad_f[:], pad_f[:], spare_f[:], ALU.add))
                dve.tensor_copy(pad_row[:], pad_f[:]).then_inc(pads_ready, 1)
                did(dve.memset(past[:], 0.0))
                did(dve.memset(before[:], 0.0))
                for e in range(E):
                    did(dve.tensor_scalar(past_t[:], number_f[:], ends[:, e:e + 1], None, ALU.is_ge))
                    did(dve.tensor_tensor(past[:], past[:], past_t[:], ALU.add))
                    did(dve.scalar_tensor_tensor(before[:], past_t[:], tiles[:, e:e + 1], before[:], ALU.mult, ALU.add))
                did(dve.tensor_tensor(sched_f[:], number_f[:], before[:], ALU.subtract))
                did(dve.tensor_scalar(sched_f[:], sched_f[:], float(P), None, ALU.mult))
                did(dve.scalar_tensor_tensor(sched_f[:], past[:], float(BUCKET), sched_f[:], ALU.mult, ALU.add))
                did(dve.tensor_copy(sched_r[:], sched_f[:]))
                did(dve.tensor_scalar(past[:], past[:], float(E - 1), None, ALU.min))
                dve.tensor_copy(sched_e[:], past[:]).then_inc(planned, 1)
                dve.wait_ge(planned, 1)
                did(dve.tensor_tensor(delta[:], ends[:], tiles[:], ALU.subtract))
                did(dve.tensor_scalar(delta[:], delta[:], float(P), None, ALU.mult))
                did(dve.tensor_tensor(delta[:], delta[:], ebase[:], ALU.subtract))
                slots = slot[:].rearrange("p t k -> p (t k)")
                did(dve.tensor_scalar(slot_e[:], slots, BUCKET.bit_length() - 1, None, ALU.logical_shift_right))
                did(dve.tensor_copy(slot_ef[:], slot_e[:]))
                did(dve.tensor_copy(slot_f[:], slots))
                for e in range(E):
                    did(dve.tensor_scalar(slot_d[:], slot_ef[:], float(e), delta[:, e:e + 1], ALU.is_equal, ALU.mult))
                    did(dve.tensor_tensor(slot_f[:], slot_f[:], slot_d[:], ALU.add))
                did(dve.tensor_copy(slots, slot_f[:]))
                dve.wait_ge(weights_loaded, 16 * 6)
                for e in range(E):
                    for kk in range(HALVES):
                        w = w2[:, e, kk * C:(kk + 1) * C]
                        dve.tensor_scalar(w, w, column("mult", 2 * e + kk), None, ALU.mult).then_inc(scaled, 1)

                def stage(name, tile, par):
                    if name == "B":
                        e = dve.value_load(sched_e[0:1, bass.ds(tile, 1)], min_val=0, max_val=E - 1)
                        dve.wait_ge(first_done, tile + 1)
                        dve.tensor_tensor(hidden[par][:], h_ps[par][:], b1[:, bass.ds(e, 1), :].rearrange("p o f -> p (o f)"),
                                          ALU.add).then_inc(hidden_ready, 1)
                        dve.wait_ge(gelu_ready, tile + 1)
                        if not isinstance(tile, int) or tile >= 2:
                            dve.wait_ge(acts_turned, tile - 1)
                        dve.tensor_tensor(acts[par][:], gelu[par][:], hidden[par][:, 0:F], ALU.mult).then_inc(acts_ready, 1)
                    elif name == "D":
                        e = dve.value_load(sched_e[0:1, bass.ds(tile, 1)], min_val=0, max_val=E - 1)
                        dve.wait_ge(second_done, tile + 1)
                        if not isinstance(tile, int) or tile >= 2:
                            dve.wait_ge(rows_stored[par], 16 * turn(tile, par))
                        dve.tensor_tensor(rows_out[par][:], o_ps[par][:, 0:C], b2[:, bass.ds(e, 1), :].rearrange("p o f -> p (o f)"),
                                          ALU.add).then_inc(out_ready, 1)

                run(dve, stage, "BD")


def phase3(nc, sb_all, sem, column, weight, slot, rows, s_fc1, s_fc2, x1_dram, x1t_dram, tile_out, out):
    with ExitStack() as ctx:
        def sb(name, shape, dt=F32):
            return sb_all(name, shape, dt, ctx)

        def ps(name, shape, dt=F32):
            return ctx.enter_context(nc.psum_tensor(name, shape, dt))

        M = FS // P
        w1 = sb("sw1", [P, HALVES, 2 * FS])
        w2 = sb("sw2", [P, M, C])
        b2 = sb("sb2", [P, C])
        xt = [sb(f"s_xt{i}", [P, HALVES, T]) for i in range(2)]
        xr = [sb(f"s_xr{i}", [P, Q, C]) for i in range(2)]
        chosen_rows = [sb(f"chosen_rows{i}", [P, Q * TOPK, C]) for i in range(2)]
        slots = [sb(f"slots{i}", [P, Q * TOPK], U32) for i in range(2)]
        wts = [sb(f"wts{i}", [P, Q * TOPK]) for i in range(2)]
        gelu = [sb(f"s_gelu{i}", [P, T]) for i in range(2)]
        acts = [sb(f"s_acts{i}", [P, M, T]) for i in range(2)]
        acc = sb("acc", [P, Q, C])
        bn = sb("s_bn", [P, Q, 6])
        mv = sb("s_mv", [P, Q, 2])
        ln = sb("s_ln", [P, 5, Q])
        result = [sb(f"result{i}", [P, Q, C]) for i in range(2)]
        gx = [[ps(f"ps_s{n}{i}", [P, T]) for i in range(2)] for n in "gx"]
        o_ps = [ps(f"ps_so{i}", [P, T]) for i in range(4)]

        loaded = sem("s_loaded")
        scaled = sem("s_scaled")
        xt_loaded = [sem(f"s_xt_loaded{i}") for i in range(2)]
        xr_loaded = [sem(f"s_xr_loaded{i}") for i in range(2)]
        slots_ready = sem("s_slots_ready")
        gathered = [sem(f"gathered{i}") for i in range(2)]
        g_done = sem("s_g_done")
        gelu_ready = sem("s_gelu_ready")
        acts_ready = sem("s_acts_ready")
        out_done = [sem(f"s_out_done{i}") for i in range(2)]
        acc_step = sem("acc_step")
        taken = sem("s_taken")
        biased = sem("biased")
        picked = sem("s_picked")
        result_ready = sem("result_ready")
        stored = [sem(f"stored{i}") for i in range(2)]
        ACC_STEPS = Q * TOPK + 2 * Q + RSQRT_STEPS

        def run(eng, body):
            with eng.Fori(0, B // 2) as n:
                for par in range(2):
                    body(n * 2 + par, n, par)

        with nc.Block() as block:
            @block.sync
            def _(sp):
                sp.dma_start(w1[:], s_fc1.rearrange("(h p) n -> p h n", p=P)).then_inc(loaded, 16)
                sp.dma_start(w2[:], s_fc2.rearrange("(m p) n -> p m n", p=P)).then_inc(loaded, 16)
                sp.dma_start(b2[:], rows[0:1, E * (2 * F + C):E * (2 * F + C) + C].partition_broadcast(P)
                             .rearrange("p o n -> p (o n)")).then_inc(loaded, 16)

                def load(j, n, par, waits=()):
                    j, at = ahead(sp, j), ahead(sp, j * T)
                    for used, value in [(used, sp.to_reg(value)) for used, value in waits]:
                        sp.wait_ge(used, value)
                    sp.dma_start(xt[par][:].rearrange("p h t -> p (h t)"), x1t_dram[bass.ds(j, 1), :, :]
                                 .rearrange("o p c -> (o p) c")).then_inc(xt_loaded[par], 16)
                    sp.dma_start(xr[par][:], x1_dram[bass.ds(at, T), :].rearrange("(q p) c -> p q c", p=P)
                                 ).then_inc(xr_loaded[par], 16)

                for par in range(2):
                    load(par, 0, par)
                with sp.Fori(1, B // 2) as n:
                    for par in range(2):
                        j = n * 2 + par
                        load(j, n, par, ((g_done, (j - 1) * M), (taken, (j - 1) * 2)))

            @block.gpsimd
            def _(pool):
                def body(j, n, par):
                    wait_apart(pool, (scaled, M), (slots_ready, j + 1))
                    for i in range(Q * TOPK):
                        pool.indirect_dma_start(out=chosen_rows[par][:, i, :], out_offset=None, in_=tile_out,
                                                in_offset=bass.IndirectOffsetOnAxis(ap=slots[par][:, i:i + 1], axis=0)
                                                ).then_inc(gathered[par], 16)
                run(pool, body)

            @block.tensor
            def _(pe):
                pe.wait_ge(loaded, 16 * 3)
                pe.wait_ge(scaled, M)

                def first(j, n, par):
                    pe.wait_ge(xt_loaded[par], 16 * (n + 1))
                    for m in range(M):
                        if m >= 2:
                            pe.wait_ge(acts_ready, j * M + m - 1)
                        elif not isinstance(j, int) or j > 0:
                            pe.wait_ge(acts_ready, j * M + m - 1)
                        for i, at in ((0, FS), (1, 0)):
                            for kk in range(HALVES):
                                last = pe.matmul(gx[i][m % 2][:], w1[:, kk, at + m * P:at + (m + 1) * P], xt[par][:, kk, :],
                                                 start=kk == 0, stop=kk == 1)
                        last.then_inc(g_done, 1)

                def second(j, n, par):
                    pe.wait_ge(acts_ready, (j + 1) * M)
                    for i in range(2):
                        if not isinstance(j, int) or j >= 2:
                            pe.wait_ge(taken, (j - 2) * 2 + i + 1)
                        for q in (2 * i, 2 * i + 1):
                            for m in range(M):
                                last = pe.matmul(o_ps[2 * par + i][:, q % 2 * C:(q % 2 + 1) * C], acts[par][:, m, q * P:(q + 1) * P],
                                                 w2[:, m, :], start=m == 0, stop=m == M - 1)
                        last.then_inc(out_done[i], 1)

                first(0, 0, 0)
                first(1, 0, 1)
                second(0, 0, 0)

                def pair(n):
                    first(n * 2, n, 0)
                    second(n * 2 - 1, n, 1)
                    first(n * 2 + 1, n, 1)
                    second(n * 2, n, 0)

                pair(1)
                with pe.Fori(2, B // 2) as n:
                    pair(n)
                second(B - 1, B // 2 - 1, 1)

            @block.scalar
            def _(act):
                act.wait_ge(scaled, M)

                def body(j, n, par):
                    for m in range(M):
                        act.wait_ge(g_done, j * M + m + 1)
                        act.activation(gelu[m % 2][:], gx[0][m % 2][:], ACT.Gelu, bias=column("s_b1", M + m)).then_inc(gelu_ready, 1)

                def store(j, n, par):
                    act.wait_ge(result_ready, j + 1)
                    act.dma_start(out[bass.ds(j * T, T), :].rearrange("(q p) c -> p q c", p=P), result[par][:]
                                  ).then_inc(stored[par], 16)

                body(0, 0, 0)
                body(1, 0, 1)
                store(0, 0, 0)

                def pair(n):
                    body(n * 2, n, 0)
                    store(n * 2 - 1, n - 1, 1)
                    body(n * 2 + 1, n, 1)
                    store(n * 2, n, 0)

                pair(1)
                with act.Fori(2, B // 2) as n:
                    pair(n)
                store(B - 1, B // 2 - 1, 1)
                for par in range(2):
                    act.wait_ge(stored[par], 16 * (B // 2))

            @block.vector
            def _(dve):
                chain = Chain(acc_step, ACC_STEPS)
                dve.wait_ge(loaded, 16 * 3)
                for m in range(M):
                    dve.tensor_scalar(w2[:, m, :], w2[:, m, :], column("s_mult", m), None, ALU.mult).then_inc(scaled, 1)

                def pick(j, n, par):
                    if not isinstance(j, int) or j >= 2:
                        dve.wait_ge(gathered[par], 16 * Q * TOPK * n)
                        dve.wait_ge(result_ready, j - 1)
                    dve.tensor_copy(wts[par][:], weight[:, bass.ds(j * Q, Q), :].rearrange("p q k -> p (q k)")).then_inc(picked, 1)
                    dve.tensor_copy(slots[par][:], slot[:, bass.ds(j * Q, Q), :].rearrange("p q k -> p (q k)")
                                    ).then_inc(slots_ready, 1)

                def values(j, n, par):
                    for m in range(M):
                        dve.wait_ge(gelu_ready, j * M + m + 1)
                        dve.scalar_tensor_tensor(acts[par][:, m, :], gx[1][m % 2][:], column("s_b1", m), gelu[m % 2][:],
                                                 ALU.add, ALU.mult).then_inc(acts_ready, 1)

                def sums(j, n, par):
                    chain.start(j)
                    dve.wait_ge(xr_loaded[par], 16 * (n + 1))
                    if not isinstance(j, int) or j >= 1:
                        dve.wait_ge(result_ready, j)
                    dve.tensor_tensor(acc[:], xr[par][:], b2[:].unsqueeze(1).to_broadcast([P, Q, C]), ALU.add).then_inc(biased, 1)
                    dve.wait_ge(biased, j + 1)
                    for i in range(2):
                        dve.wait_ge(out_done[i], j + 1)
                        dve.tensor_tensor(acc[:, 2 * i:2 * i + 2, :], o_ps[2 * par + i][:].rearrange("p (q c) -> p q c", q=2),
                                          acc[:, 2 * i:2 * i + 2, :], ALU.add).then_inc(taken, 1)
                    dve.wait_ge(taken, 2 * j + 2)
                    dve.wait_ge(gathered[par], 16 * Q * TOPK * (n + 1))
                    dve.wait_ge(picked, j + 1)
                    for k in range(TOPK):
                        for q in range(Q):
                            i = q * TOPK + k
                            chain.did(dve.scalar_tensor_tensor(acc[:, q, :], chosen_rows[par][:, i, :], wts[par][:, i:i + 1],
                                                               acc[:, q, :], ALU.mult, ALU.add))
                        chain.wait(dve)
                    for q in range(Q):
                        chain.did(dve.bn_stats(bn[:, q, :], acc[:, q, :]))
                    chain.wait_apart(dve, (scaled, M))
                    for q in range(Q):
                        chain.did(dve.bn_aggr(mv[:, q, :], bn[:, q, :]))
                    chain.wait(dve)
                    rsqrt(dve, chain, ln[:, 0, :], ln[:, 1, :], ln[:, 2, :], ln[:, 3, :], mv[:, :, 1], 1.0, LN_EPS)
                    chain.wait(dve)
                    chain.end()
                    if not isinstance(j, int) or j >= 2:
                        dve.wait_ge(stored[par], 16 * n)
                    for q in range(Q):
                        ins = dve.tensor_scalar(result[par][:, q, :], acc[:, q, :], mv[:, q, 0:1], ln[:, 0, q:q + 1],
                                                ALU.subtract, ALU.mult)
                    ins.then_inc(result_ready, 1)

                pick(0, 0, 0)
                pick(1, 0, 1)
                values(0, 0, 0)
                values(1, 0, 1)
                sums(0, 0, 0)

                def pair(n):
                    pick(n * 2, n, 0)
                    values(n * 2, n, 0)
                    sums(n * 2 - 1, n - 1, 1)
                    pick(n * 2 + 1, n, 1)
                    values(n * 2 + 1, n, 1)
                    sums(n * 2, n, 0)

                pair(1)
                with dve.Fori(2, B // 2) as n:
                    pair(n)
                sums(B - 1, B // 2 - 1, 1)


def lay_out(a):
    def halves(v):
        return np.asarray(v).reshape(-1, P).T

    cols = np.concatenate([halves(a["L0_attn_miu_x"]), halves(a["L0_attn_lambda_"]), halves(a["L0_attn_td_miu"]),
                           halves(a["L0_attn_u"]), halves(a["L0_attn_gn_gamma"]), halves(a["L0_attn_gn_beta"]),
                           halves(a["L0_ffn_s_fc1_b"]), halves(a["L0_ffn_s_geglu_mult"]), halves(a["L0_ffn_geglu_mult"])], axis=1)
    rows = np.concatenate([np.asarray(a[n]).reshape(-1) for n in ("L0_ffn_fc1_b", "L0_ffn_fc2_b", "L0_ffn_s_fc2_b")])
    arrays = {
        "x": np.asarray(a["L0_attn_x"]).reshape(B * T, C), "cols": cols, "rows": rows.reshape(1, -1),
        "wk": a["L0_attn_Wk"].T, "wv": a["L0_attn_Wv"].T, "wr": a["L0_attn_Wr"].T, "wg": a["L0_attn_Wg"].T,
        "wo": a["L0_attn_Wo"].T, "a_lora": a["L0_attn_A_lora"],
        "b_lora": np.asarray(a["L0_attn_B_lora"]).reshape(5 * LORA, C), "td_a": a["L0_attn_td_A"],
        "td_b": a["L0_attn_td_B"], "gate": a["L0_ffn_gate_w"].T,
        "fc1": np.asarray(a["L0_ffn_fc1_w"]).transpose(0, 2, 1), "fc2": np.asarray(a["L0_ffn_fc2_w"]).transpose(0, 2, 1),
        "s_fc1": a["L0_ffn_s_fc1_w"].T, "s_fc2": a["L0_ffn_s_fc2_w"].T,
    }
    return {k: np.ascontiguousarray(v) for k, v in arrays.items()}


_OUTS = [((B, T, C), "float32")]


def kernel(**inputs):
    import concourse.bacc as bacc
    from concourse.bass_utils import run_bass_kernel_spmd as run

    nc = bacc.Bacc("TRN2", target_bir_lowering=False, num_devices=1)
    arrays = {f"in_{k}": v for k, v in lay_out(inputs).items()}
    args = {k[3:]: nc.dram_tensor(k, v.shape, mybir.dt.from_np(v.dtype), kind="ExternalInput").ap()
            for k, v in arrays.items()}
    out = nc.dram_tensor("out", (B * T, C), F32, kind="ExternalOutput").ap()
    build_program(nc, out=out, **args)
    result = run(nc, [arrays], core_ids=[0])
    return result.results[0]["out"].reshape(B, T, C)
```

```python
from contextlib import ExitStack

import numpy as np

import concourse.bass as bass
from concourse import mybir

ALU = mybir.AluOpType
ACT = mybir.ActivationFunctionType
F32 = mybir.dt.float32
BF16 = mybir.dt.bfloat16
I32 = mybir.dt.int32
U32 = mybir.dt.uint32
AX_X = mybir.AxisListType.X

P = 128
B, T, C = 16, 512, 256
HALVES = C // P
H, N = 4, 64
Q = T // P
CH = 64
NCH = T // CH
LORA = 32
TDR = 64
E, TOPK = 15, 3
F, FS = 256, 512
BUCKET = B * T
TILES = B * T * TOPK // P + E
SPARE = E
ROWS = E * BUCKET + (SPARE + E) * P
GN_EPS = 1e-5 * H
LN_EPS = 1e-5
MAGIC = 0x5F3759DF
NEWTON = 3

COLS = {}
_at = 0
for _name, _n in (("miu_x", 2), ("lambda", 10), ("td_miu", 2), ("u", 2), ("gamma", 2), ("beta", 2),
                  ("s_b1", 8), ("s_mult", 4), ("mult", 2 * E)):
    COLS[_name] = _at
    _at += _n
NCOLS = _at

ORDER = (
    ("lv", 0, 0), ("p", "L", 1), ("t", "N0", -1), ("p", "Mw", 1), ("lv", 1, 0), ("t", "N1", -1), ("p", "Mk", 1),
    ("lv", 2, 0), ("p", "TA", 1), ("t", "N2", -1), ("p", "Mv", 1), ("p", "K", 1), ("lv", 3, 0),
    ("t", "N3", -1), ("p", "TB", 1), ("t", "N4", -1), ("lv", 4, 0), ("t", "O0", -1), ("p", "Mr", 1),
    ("t", "O1", -1), ("lv", 5, 0), ("p", "V", 1), ("t", "R0", -1), ("p", "Mg", 1), ("t", "R1", -1),
    ("t", "R2", -1), ("t", "R3", -1), ("p", "R", 1), ("lv", 6, 0), ("t", "R4", -1), ("t", "R5", -1),
    ("p", "G", 1), ("y", 0, 0), ("y", 1, 0), ("p", "X", 2), ("t", "R6", -1), ("y", 2, 0), ("t", "R7", -1),
)
PJ = {"X": 0, "L": 2, "Mw": 4, "Mk": 6, "TA": 8, "Mv": 9, "K": 11, "TB": 13, "Mr": 15, "V": 17,
      "Mg": 19, "R": 21, "G": 23}
PJ_USES = 25
MIX = {"w": 0, "k": 1, "v": 2, "r": 3, "g": 4}
MIX_SLOT = {"w": 0, "k": 1, "v": 0, "r": 1, "g": 0}
MIX_RANK = {"w": 0, "k": 1, "v": 2, "r": 3, "g": 4}
MS = {"KT": 0, "Y": 2, "ZT": 4, "WO": 6, "XT": 8, "GATE": 10, "RANK": 11}
MS_USES = 12


def wait(eng, sem, value):
    if isinstance(value, int) and value <= 0:
        return
    eng.wait_ge(sem, value)


def ahead(eng, value):
    return value if isinstance(value, int) else eng.snap(value)


def wait_apart(eng, constants, *waits):
    waits = [(sem, value if isinstance(value, int) else eng.to_reg(value)) for sem, value in waits]
    eng.wait_ge(*constants)
    for sem, value in waits:
        wait(eng, sem, value)


def first(step):
    return isinstance(step, int) and step == 0


class Ring:

    def __init__(self, banks, full, free, uses):
        self.banks, self.full, self.free, self.uses = banks, full, free, uses

    def count(self, step, n):
        return step * len(range(n % 2, self.uses, 2)) + n // 2

    def bank(self, n):
        return self.banks[n % 2]

    def wait_full(self, eng, step, n):
        wait(eng, self.full[n % 2], self.count(step, n) + 1)

    def wait_free(self, eng, step, n):
        wait(eng, self.free[n % 2], self.count(step, n))

    def wait_read(self, eng, step, n):
        wait(eng, self.free[n % 2], self.count(step, n) + 1)


class Chain:

    def __init__(self, sem, per):
        self.sem, self.per, self.base, self.n = sem, per, 0, 0

    def start(self, step):
        self.base, self.n = step * self.per, 0

    def did(self, instruction):
        instruction.then_inc(self.sem, 1)
        self.n += 1

    def wait(self, eng):
        eng.wait_ge(self.sem, self.base + self.n)

    def wait_apart(self, eng, constants):
        wait_apart(eng, constants, (self.sem, self.base + self.n))

    def end(self):
        assert self.n == self.per, (self.n, self.per)


def rsqrt(dve, chain, y, v, half, t, var, scale, eps):
    chain.did(dve.tensor_scalar(v, var, scale, eps, ALU.mult, ALU.add))
    chain.wait(dve)
    chain.did(dve.tensor_scalar(half, v, -0.5, None, ALU.mult))
    chain.did(dve.tensor_scalar(t.bitcast(U32), v.bitcast(U32), 1, None, ALU.logical_shift_right))
    chain.wait(dve)
    chain.did(dve.tensor_scalar(y.bitcast(I32), t.bitcast(I32), -1.0, float(MAGIC), ALU.mult, ALU.add))
    for _ in range(NEWTON):
        chain.wait(dve)
        chain.did(dve.tensor_tensor(t, y, y, ALU.mult))
        chain.wait(dve)
        chain.did(dve.tensor_tensor(t, t, half, ALU.mult))
        chain.wait(dve)
        chain.did(dve.scalar_tensor_tensor(y, t, 1.5, y, ALU.add, ALU.mult))


RSQRT_STEPS = 4 + 3 * NEWTON


def build_program(nc, x, cols, rows, wk, wv, wr, wg, wo, a_lora, b_lora, td_a, td_b, gate, fc1, fc2,
                  s_fc1, s_fc2, out):
    x1_dram = nc.dram_tensor("x1_rows", (B * T, C), F32).ap()
    x1t_dram = nc.dram_tensor("x1_columns", (B, P, HALVES * T), F32).ap()
    bucket_in = nc.dram_tensor("bucket_in", (ROWS, C), F32).ap()
    tile_out = nc.dram_tensor("tile_out", (TILES * P, C), F32).ap()

    with ExitStack() as ctx:
        def sb(name, shape, dt=F32, stack=ctx):
            return stack.enter_context(nc.sbuf_tensor(name, shape, dt))

        def sem(name):
            return ctx.enter_context(nc.semaphore(name))

        vec = sb("vec", [P, NCOLS])
        ident = sb("ident", [P, P])
        weight = sb("weight", [P, B * Q, TOPK])
        slot = sb("slot", [P, B * Q, TOPK], U32)
        count = sb("count", [P, Q + 1, E])
        ebase = sb("ebase", [P, E])

        def column(name, n):
            return vec[:, COLS[name] + n:COLS[name] + n + 1]

        with ExitStack() as both:
            experts = Experts(lambda name, shape, dt=F32: sb(name, shape, dt, both), sem)
            phase1(nc, sb, sem, column, vec, ident, weight, slot, count, ebase, x, cols, wk, wv, wr, wg, wo,
                   a_lora, b_lora, td_a, td_b, gate, x1_dram, x1t_dram, bucket_in, rows, fc1, fc2, experts)
            phase2(nc, sb, sem, ident, bucket_in, tile_out, experts)
        phase3(nc, sb, sem, column, weight, slot, rows, s_fc1, s_fc2, x1_dram, x1t_dram, tile_out, out)


class Views:

    def __init__(self, whole):
        self.whole, self.used = whole, 0

    def cut(self, rows_, *shape):
        at, self.used = self.used, self.used + int(np.prod(shape))
        assert self.used <= self.whole.shape[-1]
        names = "abcd"[:len(shape)]
        return self.whole[0:rows_, at:self.used].rearrange(f"p ({' '.join(names)}) -> p {' '.join(names)}",
                                                           **{n: size for n, size in zip(names[1:], shape[1:])})


class Experts:
    DUMMY = E * BUCKET

    def __init__(self, sb, sem):
        self.w1 = sb("w1", [P, E, HALVES * 2 * F])
        self.w2 = sb("w2", [P, E, HALVES * C])
        self.b1 = sb("b1", [P, E, 2 * F])
        self.b2 = sb("b2", [P, E, C])
        self.sched_e = sb("sched_e", [P, TILES], I32)
        self.sched_r = sb("sched_r", [P, TILES], I32)
        self.zeros = sb("zeros", [P, C])
        self.number = sb("number", [P, TILES], I32)
        self.row_i = sb("row_i", [P, E], I32)
        self.spare_i = sb("spare_i", [P, E], I32)
        self.pad_row = sb("pad_row", [P, E], U32)
        self.small = {n: sb(n, [P, E], dt) for n, dt in (
            ("row_f", F32), ("spare_f", F32), ("tiles_i", I32), ("tiles", F32), ("ends", F32), ("one_e", F32),
            ("pad_f", F32), ("pad_m", F32), ("delta", F32))}
        self.long = {n: sb(n, [P, TILES]) for n in ("number_f", "past", "past_t", "before", "sched_f")}
        self.of_slots = {n: sb(n, [P, B * Q * TOPK], dt) for n, dt in (
            ("slot_e", U32), ("slot_ef", F32), ("slot_all_f", F32), ("slot_d", F32))}
        self.w1_loaded, self.w2_loaded, self.biases_loaded = (sem(n) for n in ("w1_loaded", "w2_loaded", "biases_loaded"))
        self.numbers_made, self.zeros_made = sem("numbers_made"), sem("zeros_made")
        self.plan = sem("plan")
        self.planned, self.pads_ready, self.padded = sem("planned"), sem("pads_ready"), sem("padded")
        self.scaled = sem("scaled")

    def start(self, pool, bucket_in):
        pool.memset(self.zeros[:], 0.0).then_inc(self.zeros_made, 1)
        pool.iota(self.number[:], pattern=[[1, TILES]], base=0, channel_multiplier=0).then_inc(self.numbers_made, 1)
        pool.iota(self.row_i[:], pattern=[[0, E]], base=0, channel_multiplier=1).then_inc(self.numbers_made, 1)
        pool.iota(self.spare_i[:], pattern=[[P, E]], base=self.DUMMY + SPARE * P, channel_multiplier=1
                  ).then_inc(self.numbers_made, 1)
        pool.wait_ge(self.zeros_made, 1)
        pool.dma_start(bucket_in[self.DUMMY:self.DUMMY + SPARE * P, :].rearrange("(s p) c -> p s c", p=P),
                       self.zeros[:].unsqueeze(1).to_broadcast([P, SPARE, C])).then_inc(self.padded, 16)

    def pad(self, pool, bucket_in):
        pool.wait_ge(self.pads_ready, 1)
        for e in range(E):
            pool.indirect_dma_start(out=bucket_in, out_offset=bass.IndirectOffsetOnAxis(ap=self.pad_row[:, e:e + 1], axis=0),
                                    in_=self.zeros[:], in_offset=None).then_inc(self.padded, 16)

    def scale(self, dve, column):
        dve.wait_ge(self.w2_loaded, 16 * HALVES)
        for e in range(E):
            for kk in range(HALVES):
                w = self.w2[:, e, kk * C:(kk + 1) * C]
                dve.tensor_scalar(w, w, column("mult", 2 * e + kk), None, ALU.mult).then_inc(self.scaled, 1)

    def make_plan(self, dve, count, slot, ebase):
        small, long, of_slots = self.small, self.long, self.of_slots
        n = 0

        def did(ins):
            nonlocal n
            ins.then_inc(self.plan, 1)
            n += 1
            dve.wait_ge(self.plan, n)

        dve.wait_ge(self.numbers_made, 3)
        total = count[:, 0, :]
        did(dve.tensor_scalar(small["tiles"][:], total, float(P - 1), None, ALU.add))
        did(dve.tensor_copy(small["tiles_i"][:], small["tiles"][:]))
        did(dve.tensor_scalar(small["tiles_i"][:], small["tiles_i"][:], 7, None, ALU.arith_shift_right))
        did(dve.tensor_copy(small["tiles"][:], small["tiles_i"][:]))
        did(dve.memset(small["one_e"][:], 1.0))
        did(dve.tensor_tensor_scan(small["ends"][:], small["one_e"][:], small["tiles"][:], 0.0, ALU.mult, ALU.add))
        did(dve.tensor_copy(long["number_f"][:], self.number[:]))
        did(dve.tensor_copy(small["row_f"][:], self.row_i[:]))
        did(dve.tensor_tensor(small["pad_f"][:], small["row_f"][:], total, ALU.add))
        did(dve.tensor_scalar(small["pad_m"][:], small["tiles"][:], float(P), None, ALU.mult))
        did(dve.tensor_tensor(small["pad_m"][:], small["pad_f"][:], small["pad_m"][:], ALU.is_lt))
        did(dve.tensor_tensor(small["pad_f"][:], small["pad_f"][:], ebase[:], ALU.add))
        did(dve.tensor_copy(small["spare_f"][:], self.spare_i[:]))
        did(dve.tensor_tensor(small["pad_f"][:], small["pad_f"][:], small["spare_f"][:], ALU.subtract))
        did(dve.tensor_tensor(small["pad_f"][:], small["pad_f"][:], small["pad_m"][:], ALU.mult))
        did(dve.tensor_tensor(small["pad_f"][:], small["pad_f"][:], small["spare_f"][:], ALU.add))
        dve.tensor_copy(self.pad_row[:], small["pad_f"][:]).then_inc(self.pads_ready, 1)
        did(dve.memset(long["past"][:], 0.0))
        did(dve.memset(long["before"][:], 0.0))
        for e in range(E):
            did(dve.tensor_scalar(long["past_t"][:], long["number_f"][:], small["ends"][:, e:e + 1], None, ALU.is_ge))
            did(dve.tensor_tensor(long["past"][:], long["past"][:], long["past_t"][:], ALU.add))
            did(dve.scalar_tensor_tensor(long["before"][:], long["past_t"][:], small["tiles"][:, e:e + 1], long["before"][:], ALU.mult, ALU.add))
        did(dve.tensor_tensor(long["sched_f"][:], long["number_f"][:], long["before"][:], ALU.subtract))
        did(dve.tensor_scalar(long["sched_f"][:], long["sched_f"][:], float(P), None, ALU.mult))
        did(dve.scalar_tensor_tensor(long["sched_f"][:], long["past"][:], float(BUCKET), long["sched_f"][:], ALU.mult, ALU.add))
        did(dve.tensor_copy(self.sched_r[:], long["sched_f"][:]))
        did(dve.tensor_scalar(long["past"][:], long["past"][:], float(E - 1), None, ALU.min))
        dve.tensor_copy(self.sched_e[:], long["past"][:]).then_inc(self.planned, 1)
        dve.wait_ge(self.planned, 1)
        did(dve.tensor_tensor(small["delta"][:], small["ends"][:], small["tiles"][:], ALU.subtract))
        did(dve.tensor_scalar(small["delta"][:], small["delta"][:], float(P), None, ALU.mult))
        did(dve.tensor_tensor(small["delta"][:], small["delta"][:], ebase[:], ALU.subtract))
        slots = slot[:].rearrange("p t k -> p (t k)")
        did(dve.tensor_scalar(of_slots["slot_e"][:], slots, BUCKET.bit_length() - 1, None, ALU.logical_shift_right))
        did(dve.tensor_copy(of_slots["slot_ef"][:], of_slots["slot_e"][:]))
        did(dve.tensor_copy(of_slots["slot_all_f"][:], slots))
        for e in range(E):
            did(dve.tensor_scalar(of_slots["slot_d"][:], of_slots["slot_ef"][:], float(e), small["delta"][:, e:e + 1], ALU.is_equal, ALU.mult))
            did(dve.tensor_tensor(of_slots["slot_all_f"][:], of_slots["slot_all_f"][:], of_slots["slot_d"][:], ALU.add))
        did(dve.tensor_copy(slots, of_slots["slot_all_f"][:]))

def phase1(nc, sb_all, sem, column, vec, ident, weight, slot, count, ebase, x, cols, wk, wv, wr, wg, wo,
           a_lora, b_lora, td_a, td_b, gate, x1_dram, x1t_dram, bucket_in, rows, fc1, fc2, experts):
    with ExitStack() as ctx:
        def sb(name, shape, dt=F32):
            return sb_all(name, shape, dt, ctx)

        def ps(name, shape, dt=F32):
            return ctx.enter_context(nc.psum_tensor(name, shape, dt))

        early = Views(experts.w1[:].rearrange("p e f -> p (e f)"))
        w_r, w_g, w_o = (sb(f"w_{n}", [P, HALVES, C]) for n in "rgo")
        w_k, w_v = (early.cut(P, HALVES, C) for _ in range(2))
        w_a = early.cut(P, HALVES, 5 * LORA)
        w_b = sb("w_b", [P, C])
        w_b4 = sb("w_b4", [LORA, C])
        w_ta = early.cut(P, HALVES, TDR)
        w_tb = sb("w_tb", [TDR, C])
        w_gate = sb("w_gate", [P, HALVES, E])
        mask = sb("mask", [P, 7, CH], U32)
        half_gb = sb("half_gb", [P, 2 * HALVES])
        tri = sb("tri", [P, P], BF16)
        ones = sb("ones", [P, P], BF16)
        iota_e = sb("iota_e", [P, Q, E])
        iota_i = sb("iota_i", [P, Q * E], I32)
        ebase_i = sb("ebase_i", [P, E], I32)
        s_i, t_i, b_a, b_b, b_c, b_d = (sb(n, [P, CH], I32) for n in ("s_i", "t_i", "b_a", "b_b", "b_c", "b_d"))
        x_turn = early.cut(P, Q, C)
        xt = early.cut(P, HALVES, T + 1)
        dxa = early.cut(P, HALVES, T)
        xm = early.cut(P, HALVES, T)
        lora = early.cut(P, T)
        lora4 = early.cut(LORA, T)
        shifted = early.cut(P, HALVES, T)
        mixed = early.cut(P, 2, HALVES, T)
        tw = early.cut(TDR, T)
        ew = early.cut(P, HALVES, T)
        gate_t = early.cut(P, HALVES, T)
        late = [Views(experts.b1[:].rearrange("p e f -> p (e f)")), Views(experts.b2[:].rearrange("p e f -> p (e f)"))]
        k_, ku = ([early.cut(P, HALVES, T), late[0].cut(P, HALVES, T)] for _ in range(2))
        v_ = [early.cut(P, Q, C), late[0].cut(P, Q, C)]
        r_, d_ = ([late[0].cut(P, HALVES, T) for _ in range(2)] for _ in range(2))
        g_ = [sb(f"g{i}", [P, HALVES, T]) for i in range(2)]
        dd = late[1].cut(P, HALVES, T)
        att = late[1].cut(P, HALVES, 2, Q, CH)
        kt = late[1].cut(P, HALVES, Q, P)
        state = sb("state", [P, HALVES, NCH, N])
        yc = sb("yc", [P, Q, H, N])
        sq = sb("sq", [P, Q, H, N])
        stat = sb("stat", [P, 5, Q, H])
        zg = sb("zg", [P, HALVES, T])
        x_res = sb("x_res", [P, Q, C])
        res = sb("res", [P, Q, C])
        bn = sb("bn", [P, Q, 6])
        mv = sb("mv", [P, Q, 2])
        ln = sb("ln", [P, 5, Q])
        x1 = sb("x1", [P, Q, C])
        x1t = sb("x1t", [P, HALVES, T])
        logit = sb("logit", [P, Q, E + 1])
        prob = sb("prob", [P, Q, E + 1])
        rt = sb("rt", [P, 4, Q])
        top = sb("top", [P, Q, 8])
        top_i = sb("top_i", [P, Q, 8], U32)
        top_f = sb("top_f", [P, Q, 8])
        onehot = sb("onehot", [P, TOPK, Q * E])
        chosen = sb("chosen", [P, Q * E])
        chosen_b = sb("chosen_b", [P, Q * E], BF16)
        place = sb("place", [P, Q, E])
        picked = sb("picked", [P, TOPK, Q * E])
        slot_f = sb("slot_f", [P, Q, TOPK])
        slot_now = sb("slot_now", [P, Q, TOPK], U32)

        pj = Ring([ps(f"ps_pj{i}", [P, T]) for i in range(2)], [sem(f"pj_full{i}") for i in range(2)],
                  [sem(f"pj_free{i}") for i in range(2)], PJ_USES)
        ms = Ring([ps(f"ps_ms{i}", [P, T]) for i in range(2)], [sem(f"ms_full{i}") for i in range(2)],
                  [sem(f"ms_free{i}") for i in range(2)], MS_USES)
        lv = [[ps(f"ps_lv{i}{j}", [P, T]) for j in range(2)] for i in range(HALVES)]

        loaded = sem("loaded")
        made = sem("made")
        prep = sem("prep")
        xa_loaded = sem("xa_loaded")
        xr_loaded = sem("xr_loaded")
        dxa_done = sem("dxa_done")
        xm_ready = sem("xm_ready")
        mix_step = sem("mix_step")
        mixed_ready = sem("mixed_ready")
        ew_ready = sem("ew_ready")
        gate_ready = sem("gate_ready")
        mask_step = sem("mask_step")
        lv_full = [sem(f"lv_full{i}") for i in range(2)]
        lv_free = [sem(f"lv_free{i}") for i in range(2)]
        rkd = [sem(f"rkd{i}") for i in range(2)]
        state_step = [sem(f"state_step{i}") for i in range(2)]
        scored = sem("scored")
        norm_step = sem("norm_step")
        squared = sem("squared")
        yn_ready = sem("yn_ready")
        z_ready = sem("z_ready")
        ln_step = sem("ln_step")
        x1_ready = sem("x1_ready")
        x1_stored = sem("x1_stored")
        x1t_stored = sem("x1t_stored")
        route_step = sem("route_step")
        exp_ready = sem("exp_ready")
        chosen_ready = sem("chosen_ready")
        slots_ready = sem("slots_ready")
        scattered = sem("scattered")

        LOADS = 16 * 13
        MADE = 9
        PREP = 9
        NORM_STEPS = 3 * 2 + 1 + RSQRT_STEPS
        LN_STEPS = Q + Q + RSQRT_STEPS
        ROUTE_STEPS = 13 + 3 * TOPK + 3 * Q

        def doubled(hp, b, level):
            return rkd[hp], b * 18 + 3 * level

        def steps(eng, p_stage, lv_stage, y_stage, t_stage):
            stages = {"p": p_stage, "lv": lv_stage, "y": y_stage, "t": t_stage}

            def step(base, n):
                for kind, what, lead in ORDER:
                    if not isinstance(base, int) or 0 <= base + n + lead < B:
                        stages[kind](what, base + (n + lead), (n + lead) % 2)

            for n in range(-2, 2):
                step(0, n)
            with eng.Fori(0, (B - 4) // 2) as pair:
                for n in (2, 3):
                    step(pair * 2, n)
            for n in range(B - 2, B + 1):
                step(0, n)

        with nc.Block() as block:
            @block.sync
            def _(sp):
                for dst, src in ((vec[:], cols), (w_k[:], wk.rearrange("(h p) n -> p h n", p=P)),
                                 (w_v[:], wv.rearrange("(h p) n -> p h n", p=P)),
                                 (w_r[:], wr.rearrange("(h p) n -> p h n", p=P)),
                                 (w_g[:], wg.rearrange("(h p) n -> p h n", p=P)),
                                 (w_o[:], wo.rearrange("(h p) n -> p h n", p=P)),
                                 (w_b[:], b_lora[0:P, :]), (w_b4[:], b_lora[P:P + LORA, :]),
                                 (w_tb[:], td_b)):
                    sp.dma_start(dst, src).then_inc(loaded, 16)
                for dst, src in ((w_a[:], a_lora.rearrange("(h p) n -> p h n", p=P)),
                                 (w_ta[:], td_a.rearrange("(h p) n -> p h n", p=P)),
                                 (w_gate[:, 0, :], gate[0:P, :]), (w_gate[:, 1, :], gate[P:C, :])):
                    sp.dma_start(dst, src).then_inc(loaded, 16)

                def p_stage(what, b, par):
                    if what == "X":
                        at = ahead(sp, b * T)
                        if not first(b):
                            pj.wait_full(sp, b - 1, 1)
                        sp.dma_start(x_turn, x[bass.ds(at, T), :].rearrange("(q p) c -> p q c", p=P)
                                     ).then_inc(xa_loaded, 16)

                def lv_stage(level, b, par):
                    if level == 0 and first(b):
                        for kk in range(HALVES):
                            sp.dma_start(experts.w2[:, :, kk * C:(kk + 1) * C],
                                         fc2[:, kk * P:(kk + 1) * P, :].rearrange("e p f -> p e f")).then_inc(experts.w2_loaded, 16)

                def y_stage(what, b, par):
                    if what == 2 and isinstance(b, int) and b == B - 2:
                        for i in range(2):
                            ms.wait_full(sp, b, MS["Y"] + i)
                            pj.wait_read(sp, B - 1, PJ["G"] + i)
                        for kk in range(HALVES):
                            sp.dma_start(experts.w1[:, :, kk * 2 * F:(kk + 1) * 2 * F],
                                         fc1[:, kk * P:(kk + 1) * P, :].rearrange("e p f -> p e f")).then_inc(experts.w1_loaded, 16)

                    elif what == 2 and isinstance(b, int) and b == B - 1:
                        for i in range(2):
                            ms.wait_full(sp, b, MS["Y"] + i)
                        for at, dst in ((0, experts.b1), (E * 2 * F, experts.b2)):
                            n = E * dst.shape[2]
                            sp.dma_start(dst[:].rearrange("p e f -> p (e f)"), rows[0:1, at:at + n].partition_broadcast(P)
                                         .rearrange("p o n -> p (o n)")).then_inc(experts.biases_loaded, 16)

                def load_residual(at):
                    sp.dma_start(x_res[:], x[bass.ds(at, T), :].rearrange("(q p) c -> p q c", p=P)
                                 ).then_inc(xr_loaded, 16)

                def t_stage(what, b, par):
                    if what == "O1" and not (isinstance(b, int) and b == B - 1):
                        at = ahead(sp, b * T + T)
                        ms.wait_read(sp, b, MS["WO"] + 1)
                        load_residual(at)

                load_residual(0)
                steps(sp, p_stage, lv_stage, y_stage, t_stage)

            @block.gpsimd
            def _(pool):
                pool.iota(iota_i[:], pattern=[[0, Q], [1, E]], base=0, channel_multiplier=0).then_inc(made, 1)
                pool.iota(ebase_i[:], pattern=[[BUCKET, E]], base=0, channel_multiplier=0).then_inc(made, 1)
                pool.iota(s_i[:], pattern=[[0, CH]], base=0, channel_multiplier=1).then_inc(made, 1)
                pool.iota(t_i[:], pattern=[[1, CH]], base=0, channel_multiplier=0).then_inc(made, 1)
                pool.memset(ones[:], 1.0).then_inc(made, 1)
                pool.memset(tri[:], 1.0).then_inc(made, 1)
                pool.memset(ident[:], 0.0).then_inc(made, 1)
                pool.wait_ge(made, 7)
                pool.affine_select(out=ident[:], in_=ident[:], compare_op=ALU.not_equal, fill=1.0, base=0,
                                   pattern=[[-1, P]], channel_multiplier=1).then_inc(made, 1)
                pool.affine_select(out=tri[:], in_=tri[:], compare_op=ALU.is_gt, fill=0.0, base=0,
                                   pattern=[[1, P]], channel_multiplier=-1).then_inc(made, 1)

                def p_stage(what, b, par):
                    if what[0] != "M":
                        return
                    slot_of = MIX_SLOT[what[1]]
                    before = {"w": "G", "k": "R", "v": "TA", "r": "K", "g": "V"}[what[1]]
                    if what[1] in "vrg":
                        pj.wait_full(pool, b, PJ[before] + (before != "TA"))
                    elif not first(b):
                        pj.wait_full(pool, b - 1, PJ[before] + 1)
                    at = b * 10 + 2 * MIX_RANK[what[1]]
                    for hp in range(HALVES):
                        pj.wait_read(pool, b, PJ[what] + hp)
                        pool.tensor_tensor(mixed[:, slot_of, hp, :], shifted[:, hp, :], dxa[:, hp, :],
                                           ALU.mult).then_inc(mix_step, 1)
                    for hp in range(HALVES):
                        pool.wait_ge(mix_step, at + hp + 1)
                        pool.tensor_tensor(mixed[:, slot_of, hp, :], mixed[:, slot_of, hp, :], xt[:, hp, 1:T + 1],
                                           ALU.add).then_inc(mixed_ready, 1)

                def lv_stage(level, b, par):
                    pass

                def y_stage(what, b, par):
                    pass

                def t_stage(what, b, par):
                    if what == "R7":
                        wait_apart(pool, (made, MADE), (slots_ready, b + 1))
                        for q in range(Q):
                            for k in range(TOPK):
                                pool.indirect_dma_start(
                                    out=bucket_in, out_offset=bass.IndirectOffsetOnAxis(ap=slot_now[:, q, k:k + 1], axis=0),
                                    in_=x1[:, q, :], in_offset=None).then_inc(scattered, 16)

                experts.start(pool, bucket_in)
                steps(pool, p_stage, lv_stage, y_stage, t_stage)
                experts.pad(pool, bucket_in)
                pool.wait_ge(scattered, 16 * B * Q * TOPK)

            @block.tensor
            def _(pe):
                pe.wait_ge(loaded, LOADS)
                pe.wait_ge(made, MADE)
                pe.wait_ge(prep, PREP)

                def p_stage(what, b, par):
                    n = PJ[what]
                    if what == "X":
                        pe.wait_ge(xa_loaded, 16 * (b + 1))
                        for hp in range(HALVES):
                            pj.wait_free(pe, b, n + hp)
                            for q in range(Q):
                                last = pe.transpose(pj.bank(n + hp)[:, q * P:(q + 1) * P],
                                                    x_turn[:, q, hp * P:(hp + 1) * P], ident[:])
                            last.then_inc(pj.full[(n + hp) % 2], 1)
                    elif what == "L":
                        pe.wait_ge(xm_ready, 2 * (b + 1))
                        for i, (rows_, first) in enumerate(((P, 0), (LORA, P))):
                            pj.wait_free(pe, b, n + i)
                            for hp in range(HALVES):
                                last = pe.matmul(pj.bank(n + i)[0:rows_, :], w_a[:, hp, first:first + rows_],
                                                 xm[:, hp, :], start=hp == 0, stop=hp == 1)
                            last.then_inc(pj.full[(n + i) % 2], 1)
                    elif what[0] == "M":
                        f = MIX[what[1]]
                        for hp in range(HALVES):
                            pj.wait_free(pe, b, n + hp)
                            wt, act_ = (w_b, lora) if f < 4 else (w_b4, lora4)
                            at = LORA * f if f < 4 else 0
                            last = pe.matmul(pj.bank(n + hp)[:], wt[at:at + LORA, hp * P:(hp + 1) * P],
                                             act_[at:at + LORA, :], start=True, stop=True)
                            last.then_inc(pj.full[(n + hp) % 2], 1)
                    elif what == "TA":
                        pe.wait_ge(mixed_ready, b * 10 + 2)
                        pj.wait_free(pe, b, n)
                        for hp in range(HALVES):
                            last = pe.matmul(pj.bank(n)[0:TDR, :], w_ta[:, hp, :], mixed[:, 0, hp, :],
                                             start=hp == 0, stop=hp == 1)
                        last.then_inc(pj.full[n % 2], 1)
                    elif what == "TB":
                        pj.wait_read(pe, b, PJ["TA"])
                        for hp in range(HALVES):
                            pj.wait_free(pe, b, n + hp)
                            last = pe.matmul(pj.bank(n + hp)[:], w_tb[:, hp * P:(hp + 1) * P], tw[:],
                                             start=True, stop=True)
                            last.then_inc(pj.full[(n + hp) % 2], 1)
                    elif what == "V":
                        pe.wait_ge(mixed_ready, b * 10 + 2 * MIX_RANK["v"] + 2)
                        for i in range(2):
                            pj.wait_free(pe, b, n + i)
                            for j in range(2):
                                q = 2 * i + j
                                for hp in range(HALVES):
                                    last = pe.matmul(pj.bank(n + i)[:, j * C:(j + 1) * C],
                                                     mixed[:, 0, hp, q * P:(q + 1) * P], w_v[:, hp, :],
                                                     start=hp == 0, stop=hp == 1)
                            last.then_inc(pj.full[(n + i) % 2], 1)
                    else:
                        f = what.lower()
                        w = {"k": w_k, "r": w_r, "g": w_g}[f]
                        pe.wait_ge(mixed_ready, b * 10 + 2 * MIX_RANK[f] + 2)
                        for hp in range(HALVES):
                            pj.wait_free(pe, b, n + hp)
                            for kk in range(HALVES):
                                last = pe.matmul(pj.bank(n + hp)[:], w[:, kk, hp * P:(hp + 1) * P],
                                                 mixed[:, MIX_SLOT[f], kk, :], start=kk == 0, stop=kk == 1)
                            last.then_inc(pj.full[(n + hp) % 2], 1)

                def lv_stage(level, b, par):
                    if level == 0:
                        for i in range(2):
                            pj.wait_read(pe, b, PJ["R"] + i)
                    left = ku[par] if level == 0 else k_[par]
                    for hp in range(HALVES):
                        ready = [doubled(hp, b, level - 1)] if level >= 2 else []
                        wait_apart(pe, (prep, PREP), (lv_free[hp], b * 8 + level), *ready)
                        for q in range(Q):
                            for h2, p2 in ((0, 0), (1, 1), (0, 1), (1, 0)):
                                t0 = (2 * q + p2) * CH
                                rows_ = slice(h2 * N, h2 * N + N)
                                last = pe.matmul(lv[hp][h2][p2 * CH:(p2 + 1) * CH, q * CH:(q + 1) * CH],
                                                 left[rows_, hp, t0:t0 + CH], r_[par][rows_, hp, t0:t0 + CH],
                                                 start=True, stop=True)
                        last.then_inc(lv_full[hp], 1)

                def y_stage(what, b, par):
                    if what == 0:
                        for hp in range(HALVES):
                            ms.wait_free(pe, b, hp)
                            pe.wait_ge(*doubled(hp, b, 6))
                            for q in range(Q):
                                last = pe.transpose(ms.bank(hp)[:, q * P:(q + 1) * P], k_[par][:, hp, q * P:(q + 1) * P],
                                                    ident[:])
                            last.then_inc(ms.full[hp], 1)
                    elif what == 1:
                        for i in range(2):
                            pj.wait_read(pe, b, PJ["V"] + i)
                        for hp in range(HALVES):
                            wait_apart(pe, (prep, PREP), (ms.free[hp], ms.count(b, hp) + 1), (lv_free[hp], b * 8 + 7))
                            for c in range(NCH - 1):
                                for h2 in range(2):
                                    p2 = c % 2
                                    rows_ = slice(p2 * CH, p2 * CH + CH)
                                    at = (2 * hp + h2) * N
                                    last = pe.matmul(lv[hp][p2][h2 * N:(h2 + 1) * N, c // 2 * N:(c // 2 + 1) * N],
                                                     kt[rows_, hp, c // 2, h2 * N:(h2 + 1) * N],
                                                     v_[par][rows_, c // 2, at:at + N], start=True, stop=True)
                            last.then_inc(lv_full[hp], 1)
                        n = MS["Y"]
                        for h2 in range(2):
                            for hp in range(HALVES):
                                for q in range(Q):
                                    for p2 in range(2):
                                        rows_ = slice(p2 * CH, (p2 + 1) * CH)
                                        h = 2 * hp + h2
                                        last = pe.matmul(ms.bank(n + h2)[rows_, (hp * Q + q) * N:(hp * Q + q + 1) * N],
                                                         att[rows_, hp, h2, q, :], v_[par][rows_, q, h * N:(h + 1) * N],
                                                         start=hp == 0 and q == 0, stop=False, skip_group_check=True)
                        last.then_inc(scored, 1)
                    else:
                        n = MS["Y"]
                        wait_apart(pe, (prep, PREP), (scored, b + 1), *((lv_free[hp], b * 8 + 8) for hp in range(HALVES)))
                        for hp in range(HALVES):
                            for q in range(Q):
                                for h2, p2 in ((0, 0), (1, 1), (0, 1), (1, 0)):
                                    c = 2 * q + p2
                                    rows_ = slice(h2 * N, h2 * N + N)
                                    last = pe.matmul(ms.bank(n + h2)[p2 * CH:(p2 + 1) * CH, (hp * Q + q) * N:(hp * Q + q + 1) * N],
                                                     r_[par][rows_, hp, c * CH:(c + 1) * CH], state[rows_, hp, c, :],
                                                     start=False, stop=hp == 1 and q == Q - 1, skip_group_check=True)
                                    if hp == 1 and q == Q - 1 and (h2, p2) in ((0, 1), (1, 0)):
                                        last.then_inc(ms.full[(n + h2) % 2], 1)

                def t_stage(what, b, par):
                    if what == "N3":
                        pe.wait_ge(yn_ready, b + 1)
                        for hp in range(HALVES):
                            n = MS["ZT"] + hp
                            ms.wait_free(pe, b, n)
                            for q in range(Q):
                                last = pe.transpose(ms.bank(n)[:, q * P:(q + 1) * P], yc[:, q, 2 * hp:2 * hp + 2, :], ident[:])
                            last.then_inc(ms.full[n % 2], 1)
                    elif what == "O0":
                        pe.wait_ge(z_ready, 2 * b + 2)
                        for i in range(2):
                            n = MS["WO"] + i
                            ms.wait_free(pe, b, n)
                            for j in range(2):
                                q = 2 * i + j
                                for hp in range(HALVES):
                                    last = pe.matmul(ms.bank(n)[:, j * C:(j + 1) * C], zg[:, hp, q * P:(q + 1) * P],
                                                     w_o[:, hp, :], start=hp == 0, stop=hp == 1)
                            last.then_inc(ms.full[n % 2], 1)
                    elif what == "R0":
                        pe.wait_ge(x1_ready, b + 1)
                        for hp in range(HALVES):
                            n = MS["XT"] + hp
                            ms.wait_free(pe, b, n)
                            for q in range(Q):
                                last = pe.transpose(ms.bank(n)[:, q * P:(q + 1) * P], x1[:, q, hp * P:(hp + 1) * P], ident[:])
                            last.then_inc(ms.full[n % 2], 1)
                    elif what == "R1":
                        n = MS["GATE"]
                        ms.wait_read(pe, b, MS["XT"] + 1)
                        ms.wait_free(pe, b, n)
                        for q in range(Q):
                            for hp in range(HALVES):
                                last = pe.matmul(ms.bank(n)[:, q * (E + 1):q * (E + 1) + E], x1t[:, hp, q * P:(q + 1) * P],
                                                 w_gate[:, hp, :], start=hp == 0, stop=hp == 1)
                        last.then_inc(ms.full[n % 2], 1)
                    elif what == "R4":
                        n = MS["RANK"]
                        pe.wait_ge(chosen_ready, b + 1)
                        ms.wait_free(pe, b, n)
                        pe.matmul(ms.bank(n)[:, 0:Q * E], tri[:], chosen_b[:], start=True, stop=True)
                        last = pe.matmul(ms.bank(n)[:, Q * E:2 * Q * E], ones[:], chosen_b[:], start=True, stop=True)
                        last.then_inc(ms.full[n % 2], 1)

                steps(pe, p_stage, lv_stage, y_stage, t_stage)

            @block.scalar
            def _(act):
                act.wait_ge(loaded, LOADS)
                act.wait_ge(prep, PREP)

                def p_stage(what, b, par):
                    n = PJ[what]

                    def read(i, instruction):
                        instruction.then_inc(pj.free[(n + i) % 2], 1)

                    if what == "X":
                        wait(act, mixed_ready, b * 10)
                        for hp in range(HALVES):
                            pj.wait_full(act, b, n + hp)
                            read(hp, act.activation(xt[:, hp, 1:T + 1], pj.bank(n + hp)[:], ACT.Copy))
                    elif what == "L":
                        for i, dst in enumerate((lora[:], lora4[:])):
                            pj.wait_full(act, b, n + i)
                            read(i, act.activation(dst, pj.bank(n + i)[0:dst.shape[0], :], ACT.Tanh))
                    elif what[0] == "M":
                        f = MIX[what[1]]
                        for hp in range(HALVES):
                            pj.wait_full(act, b, n + hp)
                            wait(act, mix_step, b * 10 + 2 * f + hp - 1)
                            read(hp, act.activation(shifted[:, hp, :], pj.bank(n + hp)[:], ACT.Identity,
                                                    bias=column("lambda", 2 * f + hp)))
                    elif what == "TA":
                        pj.wait_full(act, b, n)
                        read(0, act.activation(tw[:], pj.bank(n)[0:TDR, :], ACT.Tanh))
                    elif what == "TB":
                        if not (isinstance(b, int) and b < 2):
                            ms.wait_full(act, b - 2, MS["Y"] + 1)
                        for hp in range(HALVES):
                            pj.wait_full(act, b, n + hp)
                            act.activation(ew[:, hp, :], pj.bank(n + hp)[:], ACT.Exp, bias=column("td_miu", hp)
                                           ).then_inc(ew_ready, 1)
                            act.wait_ge(ew_ready, 2 * b + hp + 1)
                            read(hp, act.activation(d_[par][:, hp, :], ew[:, hp, :], ACT.Exp, scale=-1.0))
                    elif what == "K":
                        if not (isinstance(b, int) and b < 2):
                            for i in range(2):
                                ms.wait_full(act, b - 2, MS["Y"] + i)
                        for hp in range(HALVES):
                            pj.wait_full(act, b, n + hp)
                            act.activation(k_[par][:, hp, :], pj.bank(n + hp)[:], ACT.Copy)
                            read(hp, act.activation(ku[par][:, hp, :], pj.bank(n + hp)[:], ACT.Copy, scale=column("u", hp)))
                    elif what == "R":
                        for hp in range(HALVES):
                            pj.wait_full(act, b, n + hp)
                            read(hp, act.activation(r_[par][:, hp, :], pj.bank(n + hp)[:], ACT.Copy))
                    elif what == "V":
                        for i in range(2):
                            pj.wait_full(act, b, n + i)
                            read(i, act.activation(v_[par][:, 2 * i:2 * i + 2, :], pj.bank(n + i)[:].rearrange("p (q c) -> p q c", q=2),
                                                   ACT.Copy))
                    elif what == "G":
                        for hp in range(HALVES):
                            pj.wait_full(act, b, n + hp)
                            act.activation(gate_t[:, hp, :], pj.bank(n + hp)[:], ACT.Tanh, scale=0.5).then_inc(gate_ready, 1)

                def lv_stage(level, b, par):
                    pass

                def y_stage(what, b, par):
                    if what == 0:
                        for hp in range(HALVES):
                            ms.wait_full(act, b, hp)
                            act.activation(kt[:, hp, :, :], ms.bank(hp)[:].rearrange("p (q c) -> p q c", q=Q), ACT.Copy
                                           ).then_inc(ms.free[hp], 1)

                def t_stage(what, b, par):
                    if what in ("N0", "N1"):
                        h2 = int(what[1])
                        ms.wait_read(act, b, MS["Y"] + h2)
                        act.activation(sq[:, :, h2::2, :], yc[:, :, h2::2, :], ACT.Square).then_inc(squared, 1)
                    elif what == "N3":
                        for hp in range(HALVES):
                            n = MS["ZT"] + hp
                            ms.wait_full(act, b, n)
                            act.activation(zg[:, hp, :], ms.bank(n)[:], ACT.Identity, bias=half_gb[:, 2 + hp:3 + hp],
                                           scale=half_gb[:, hp:hp + 1]).then_inc(ms.free[n % 2], 1)
                    elif what == "R0":
                        wait(act, x1t_stored, 16 * b)
                        for hp in range(HALVES):
                            n = MS["XT"] + hp
                            ms.wait_full(act, b, n)
                            act.activation(x1t[:, hp, :], ms.bank(n)[:], ACT.Copy).then_inc(ms.free[n % 2], 1)
                        act.wait_ge(x1_ready, b + 1)
                        act.dma_start(x1_dram[bass.ds(b * T, T), :].rearrange("(q p) c -> p q c", p=P), x1[:]
                                      ).then_inc(x1_stored, 16)
                        for hp in range(HALVES):
                            ms.wait_read(act, b, MS["XT"] + hp)
                        act.dma_start(x1t_dram[bass.ds(b, 1), :, :].rearrange("o p c -> (o p) c"),
                                      x1t[:].rearrange("p h t -> p (h t)")).then_inc(x1t_stored, 16)
                    elif what == "R2":
                        ms.wait_read(act, b, MS["GATE"])
                        act.activation(prob[:, :, 0:E], logit[:, :, 0:E], ACT.Exp).then_inc(exp_ready, 1)

                steps(act, p_stage, lv_stage, y_stage, t_stage)
                act.wait_ge(x1_stored, 16 * B)
                act.wait_ge(x1t_stored, 16 * B)

            @block.vector
            def _(dve):
                norm, lnc, route = Chain(norm_step, NORM_STEPS), Chain(ln_step, LN_STEPS), Chain(route_step, ROUTE_STEPS)
                dve.memset(xt[:, :, 0:1], 0.0).then_inc(prep, 1)
                dve.memset(att[:], 0.0).then_inc(prep, 1)
                dve.memset(count[:], 0.0).then_inc(prep, 1)
                dve.memset(state[:, :, 0, :], 0.0).then_inc(prep, 1)
                dve.wait_ge(loaded, LOADS)
                dve.tensor_scalar(half_gb[:], vec[:, COLS["gamma"]:COLS["gamma"] + 4], 0.5, None, ALU.mult).then_inc(prep, 1)
                dve.wait_ge(made, MADE)
                dve.tensor_copy(iota_e[:].rearrange("p q e -> p (q e)"), iota_i[:]).then_inc(prep, 1)
                dve.tensor_copy(ebase[:], ebase_i[:]).then_inc(prep, 1)
                dve.tensor_scalar(s_i[:], s_i[:], CH - 1, None, ALU.bitwise_and).then_inc(prep, 1)
                dve.wait_ge(prep, 8)
                dve.tensor_tensor(mask[:, 0, :], s_i[:], t_i[:], ALU.is_equal).then_inc(prep, 1)
                mk = 0
                for level in range(1, 7):
                    m = 1 << (level - 1)
                    dve.tensor_scalar(b_a[:], s_i[:], 2 * m - 1, None, ALU.bitwise_or).then_inc(mask_step, 1)
                    dve.tensor_scalar(b_b[:], t_i[:], 2 * m - 1, None, ALU.bitwise_or).then_inc(mask_step, 1)
                    dve.tensor_scalar(b_c[:], s_i[:], m, None, ALU.bitwise_and).then_inc(mask_step, 1)
                    dve.tensor_scalar(b_d[:], t_i[:], m, None, ALU.bitwise_and).then_inc(mask_step, 1)
                    dve.wait_ge(mask_step, mk + 4)
                    dve.tensor_tensor(b_a[:], b_a[:], b_b[:], ALU.is_equal).then_inc(mask_step, 1)
                    dve.tensor_tensor(b_c[:], b_d[:], b_c[:], ALU.is_gt).then_inc(mask_step, 1)
                    dve.wait_ge(mask_step, mk + 6)
                    dve.tensor_tensor(mask[:, level, :], b_a[:], b_c[:], ALU.mult).then_inc(mask_step, 1)
                    mk += 7
                    dve.wait_ge(mask_step, mk)
                dve.wait_ge(prep, PREP)

                def p_stage(what, b, par):
                    if what == "X":
                        for hp in range(HALVES):
                            pj.wait_read(dve, b, PJ["X"] + hp)
                        dve.tensor_tensor(dxa[:], xt[:, :, 0:T], xt[:, :, 1:T + 1], ALU.subtract).then_inc(dxa_done, 1)
                        dve.wait_ge(dxa_done, b + 1)
                        for hp in range(HALVES):
                            if not first(b):
                                pj.wait_full(dve, b - 1, PJ["L"] + 1)
                            dve.scalar_tensor_tensor(xm[:, hp, :], dxa[:, hp, :], column("miu_x", hp), xt[:, hp, 1:T + 1],
                                                     ALU.mult, ALU.add).then_inc(xm_ready, 1)
                    elif what == "G":
                        n = PJ[what]
                        wait(dve, z_ready, 2 * (b - 1)) if not (isinstance(b, int) and b < 2) else None
                        for hp in range(HALVES):
                            dve.wait_ge(gate_ready, 2 * b + hp + 1)
                            dve.scalar_tensor_tensor(g_[par][:, hp, :], gate_t[:, hp, :], 1.0, pj.bank(n + hp)[:], ALU.add,
                                                     ALU.mult).then_inc(pj.free[(n + hp) % 2], 1)

                def lv_stage(level, b, par):
                    if level == 0:
                        if isinstance(b, int) and b == 1:
                            experts.scale(dve, column)
                        for hp in range(HALVES):
                            pj.wait_read(dve, b, PJ["R"] + hp)
                    for hp in range(HALVES):
                        wait_apart(dve, (prep, PREP), (lv_full[hp], b * 8 + level + 1))
                        for h2 in range(2):
                            ins = dve.copy_predicated(att[:, hp, h2, :, :], mask[:, level, :].unsqueeze(1).to_broadcast([P, Q, CH]),
                                                      lv[hp][h2][:, 0:Q * CH].rearrange("p (q t) -> p q t", t=CH))
                        ins.then_inc(lv_free[hp], 1)
                        if level:
                            m = 1 << (level - 1)
                            nb = T // (2 * m)
                            if level == 1:
                                d_in = d_[par][:, hp, :]
                            else:
                                at = T - (T >> (level - 2))
                                d_in = dd[:, hp, at:at + T // m]
                                dve.wait_ge(*doubled(hp, b, level - 1))
                            d_in = d_in.rearrange("p (n two) -> p n two", two=2)
                            at = T - (T >> (level - 1))
                            dve.tensor_tensor(dd[:, hp, at:at + nb], d_in[:, :, 0], d_in[:, :, 1], ALU.mult).then_inc(rkd[hp], 1)
                            rv = r_[par][:, hp, :].rearrange("p (n two m) -> p n two m", two=2, m=m)[:, :, 1, :]
                            kv = k_[par][:, hp, :].rearrange("p (n two m) -> p n two m", two=2, m=m)[:, :, 0, :]
                            dve.tensor_tensor(rv, rv, d_in[:, :, 0].unsqueeze(2).to_broadcast([P, nb, m]), ALU.mult
                                              ).then_inc(rkd[hp], 1)
                            dve.tensor_tensor(kv, kv, d_in[:, :, 1].unsqueeze(2).to_broadcast([P, nb, m]), ALU.mult
                                              ).then_inc(rkd[hp], 1)

                def y_stage(what, b, par):
                    if what == 1:
                        for c in range(NCH - 1):
                            for hp in range(HALVES):
                                if c == 0:
                                    dve.wait_ge(lv_full[hp], b * 8 + 8)
                                    ins = dve.tensor_copy(state[:, hp, 1, :], lv[hp][0][:, 0:N])
                                else:
                                    at = T - (T >> 5) + c
                                    if c == 1:
                                        dve.wait_ge(*doubled(hp, b, 6))
                                    dve.wait_ge(state_step[hp], b * 6 + c)
                                    ins = dve.scalar_tensor_tensor(state[:, hp, c + 1, :], state[:, hp, c, :],
                                                                   dd[:, hp, at:at + 1], lv[hp][c % 2][:, c // 2 * N:(c // 2 + 1) * N],
                                                                   ALU.mult, ALU.add)
                                ins.then_inc(lv_free[hp] if c == NCH - 2 else state_step[hp], 1)

                def did(ins):
                    route.did(ins)
                    route.wait_apart(dve, (prep, PREP))

                def t_stage(what, b, par):
                    if what in ("N0", "N1"):
                        h2 = int(what[1])
                        if h2 == 0:
                            norm.start(b)
                        ms.wait_full(dve, b, MS["Y"] + h2)
                        for hp in range(HALVES):
                            yv = ms.bank(h2)[:, hp * Q * N:(hp + 1) * Q * N].rearrange("p (q n) -> p q n", n=N)
                            norm.did(dve.tensor_reduce(stat[:, 0, :, 2 * hp + h2], yv, AX_X, ALU.add))
                        norm.wait(dve)
                        norm.did(dve.tensor_scalar(stat[:, 0, :, h2::2], stat[:, 0, :, h2::2], 1.0 / N, None, ALU.mult))
                        norm.wait(dve)
                        for hp in range(HALVES):
                            yv = ms.bank(h2)[:, hp * Q * N:(hp + 1) * Q * N].rearrange("p (q n) -> p q n", n=N)
                            ins = dve.tensor_tensor(yc[:, :, 2 * hp + h2, :], yv,
                                                    stat[:, 0, :, 2 * hp + h2].unsqueeze(2).to_broadcast([P, Q, N]), ALU.subtract)
                        ins.then_inc(ms.free[h2], 1)
                    elif what == "N2":
                        dve.wait_ge(squared, 2 * b + 2)
                        norm.did(dve.tensor_reduce(stat[:, 1, :, :], sq[:], AX_X, ALU.add))
                        norm.wait(dve)
                        rsqrt(dve, norm, *(stat[:, i, :, :].rearrange("p q h -> p (q h)") for i in (0, 2, 3, 4, 1)),
                              1.0 / N, GN_EPS)
                        norm.wait(dve)
                        norm.end()
                        ycv = yc[:].rearrange("p q h n -> p (q h) n")
                        dve.tensor_tensor(ycv, ycv, stat[:, 0, :, :].rearrange("p q h -> p (q h)").unsqueeze(2).to_broadcast([P, Q * H, N]), ALU.mult
                                          ).then_inc(yn_ready, 1)
                    elif what == "N4":
                        for hp in range(HALVES):
                            ms.wait_read(dve, b, MS["ZT"] + hp)
                            dve.tensor_tensor(zg[:, hp, :], zg[:, hp, :], g_[par][:, hp, :], ALU.mult).then_inc(z_ready, 1)
                    elif what == "O1":
                        lnc.start(b)
                        dve.wait_ge(xr_loaded, 16 * (b + 1))
                        for i in range(2):
                            n = MS["WO"] + i
                            ms.wait_full(dve, b, n)
                            dve.tensor_tensor(res[:, 2 * i:2 * i + 2, :], ms.bank(n)[:].rearrange("p (q c) -> p q c", q=2),
                                              x_res[:, 2 * i:2 * i + 2, :], ALU.add).then_inc(ms.free[n % 2], 1)
                        for i in range(2):
                            ms.wait_read(dve, b, MS["WO"] + i)
                        for q in range(Q):
                            lnc.did(dve.bn_stats(bn[:, q, :], res[:, q, :]))
                        for q in range(Q):
                            if q == 0:
                                lnc.wait_apart(dve, (prep, PREP))
                            lnc.did(dve.bn_aggr(mv[:, q, :], bn[:, q, :]))
                        lnc.wait(dve)
                        rsqrt(dve, lnc, ln[:, 0, :], ln[:, 1, :], ln[:, 2, :], ln[:, 3, :], mv[:, :, 1], 1.0, LN_EPS)
                        lnc.wait(dve)
                        lnc.end()
                        wait(dve, x1_stored, 16 * b)
                        wait(dve, scattered, 16 * Q * TOPK * b)
                        for q in range(Q):
                            ins = dve.tensor_scalar(x1[:, q, :], res[:, q, :], mv[:, q, 0:1], ln[:, 0, q:q + 1],
                                                    ALU.subtract, ALU.mult)
                        ins.then_inc(x1_ready, 1)
                    elif what == "R2":
                        route.start(b)
                        n = MS["GATE"]
                        ms.wait_full(dve, b, n)
                        gates = ms.bank(n)[:, 0:Q * (E + 1)].rearrange("p (q e) -> p q e", q=Q)[:, :, 0:E]
                        did(dve.tensor_reduce(rt[:, 0, :], gates, AX_X, ALU.max))
                        dve.tensor_tensor(logit[:, :, 0:E], gates, rt[:, 0, :].unsqueeze(2).to_broadcast([P, Q, E]),
                                          ALU.subtract).then_inc(ms.free[n % 2], 1)
                    elif what == "R3":
                        dve.wait_ge(exp_ready, b + 1)
                        did(dve.tensor_reduce(rt[:, 1, :], prob[:, :, 0:E], AX_X, ALU.add))
                        did(dve.reciprocal(rt[:, 2, :], rt[:, 1, :]))
                        did(dve.tensor_tensor(prob[:, :, 0:E], prob[:, :, 0:E],
                                              rt[:, 2, :].unsqueeze(2).to_broadcast([P, Q, E]), ALU.mult))
                        for q in range(Q):
                            route.did(dve.max(top[:, q, :], prob[:, q, 0:E]))
                        route.wait_apart(dve, (prep, PREP))
                        for q in range(Q):
                            route.did(dve.max_index(top_i[:, q, :], top[:, q, :], prob[:, q, 0:E]))
                        did(dve.tensor_reduce(rt[:, 1, :], top[:, :, 0:TOPK], AX_X, ALU.add))
                        did(dve.tensor_scalar(rt[:, 1, :], rt[:, 1, :], 1e-20, None, ALU.add))
                        did(dve.reciprocal(rt[:, 2, :], rt[:, 1, :]))
                        did(dve.tensor_tensor(weight[:, bass.ds(b * Q, Q), :], top[:, :, 0:TOPK],
                                              rt[:, 2, :].unsqueeze(2).to_broadcast([P, Q, TOPK]), ALU.mult))
                        did(dve.tensor_copy(top_f[:], top_i[:]))
                        for k in range(TOPK):
                            route.did(dve.tensor_tensor(onehot[:, k, :].rearrange("p (q e) -> p q e", q=Q), iota_e[:],
                                                        top_f[:, :, k:k + 1].to_broadcast([P, Q, E]), ALU.is_equal))
                        route.wait(dve)
                        did(dve.tensor_tensor(chosen[:], onehot[:, 0, :], onehot[:, 1, :], ALU.add))
                        dve.tensor_tensor(chosen_b[:], chosen[:], onehot[:, 2, :], ALU.add).then_inc(chosen_ready, 1)
                    elif what == "R5":
                        n = MS["RANK"]
                        ms.wait_full(dve, b, n)
                        sums = ms.bank(n)[:, Q * E:2 * Q * E].rearrange("p (q e) -> p q e", q=Q)
                        for q in range(Q):
                            did(dve.tensor_tensor(count[:, q + 1, :], count[:, q, :], sums[:, q, :], ALU.add))
                        dve.tensor_tensor(place[:], ms.bank(n)[:, 0:Q * E].rearrange("p (q e) -> p q e", q=Q),
                                          count[:, 0:Q, :], ALU.add).then_inc(ms.free[n % 2], 1)
                    elif what == "R6":
                        ms.wait_read(dve, b, MS["RANK"])
                        did(dve.tensor_tensor(place[:], place[:], ebase[:].unsqueeze(1).to_broadcast([P, Q, E]), ALU.add))
                        for k in range(TOPK):
                            route.did(dve.tensor_tensor(picked[:, k, :], onehot[:, k, :], place[:].rearrange("p q e -> p (q e)"),
                                                        ALU.mult))
                        did(dve.tensor_copy(count[:, 0, :], count[:, Q, :]))
                        for k in range(TOPK):
                            route.did(dve.tensor_reduce(slot_f[:, :, k], picked[:, k, :].rearrange("p (q e) -> p q e", q=Q),
                                                        AX_X, ALU.add))
                        route.wait(dve)
                        did(dve.tensor_copy(slot[:, bass.ds(b * Q, Q), :], slot_f[:]))
                        wait(dve, scattered, 16 * Q * TOPK * b)
                        dve.tensor_copy(slot_now[:], slot_f[:]).then_inc(slots_ready, 1)
                        route.end()

                steps(dve, p_stage, lv_stage, y_stage, t_stage)
                experts.make_plan(dve, count, slot, ebase)


def phase2(nc, sb_all, sem, ident, bucket_in, tile_out, experts):
    with ExitStack() as ctx:
        def sb(name, shape, dt=F32):
            return sb_all(name, shape, dt, ctx)

        def ps(name, shape, dt=F32):
            return ctx.enter_context(nc.psum_tensor(name, shape, dt))

        w1, w2, b1, b2, sched_e, sched_r = (experts.w1, experts.w2, experts.b1, experts.b2, experts.sched_e,
                                            experts.sched_r)
        rows_in = [sb(f"rows_in{i}", [P, C]) for i in range(2)]
        rows_t = [sb(f"rows_t{i}", [P, HALVES, P]) for i in range(2)]
        hidden = [sb(f"hidden{i}", [P, 2 * F]) for i in range(2)]
        gelu = [sb(f"gelu{i}", [P, F]) for i in range(2)]
        acts = [sb(f"acts{i}", [P, F]) for i in range(2)]
        acts_t = [sb(f"acts_t{i}", [P, HALVES, P]) for i in range(2)]
        rows_out = [sb(f"rows_out{i}", [P, C]) for i in range(2)]
        xt_ps = [ps(f"ps_xt{i}", [P, T]) for i in range(2)]
        h_ps = [ps(f"ps_h{i}", [P, T]) for i in range(2)]
        at_ps = [ps(f"ps_at{i}", [P, T]) for i in range(2)]
        o_ps = [ps(f"ps_o{i}", [P, T]) for i in range(2)]

        rows_loaded = [sem(f"rows_loaded{i}") for i in range(2)]
        rows_stored = [sem(f"rows_stored{i}") for i in range(2)]
        turned = sem("turned")
        rows_t_ready = sem("rows_t_ready")
        first_done = sem("first_done")
        hidden_ready = sem("hidden_ready")
        gelu_ready = sem("gelu_ready")
        acts_ready = sem("acts_ready")
        acts_turned = sem("acts_turned")
        acts_t_ready = sem("acts_t_ready")
        second_done = sem("second_done")
        out_ready = sem("out_ready")

        UNROLL = 4

        def run(eng, engine, stage, order, table, of):
            limit = E - 1 if table is sched_e else ROWS - P

            def load(tile, n):
                return nc.values_load_multi_w_load_instructions(
                    table[0:1, bass.ds(tile, n)], engines=(engine,), min_val=0, max_val=limit,
                    skip_runtime_bounds_check_because="the schedule holds experts up to E - 1 and rows of the buckets")[1]

            def one(i, par, value):
                for name, lead in order:
                    if not isinstance(i, int) or 0 <= i + lead < TILES:
                        stage(name, i + lead, (par + lead) % 2, value(lead) if name in of else None)

            def peeled(steps):
                for i in steps:
                    one(i, i % 2, lambda lead, i=i: load(i + lead, 1)[0])

            first_, loops = 3, (TILES - 5) // UNROLL
            peeled(range(-2, first_))
            leads = [lead for name, lead in order if name in of]
            with eng.Fori(0, loops) as n:
                if leads:
                    lowest = min(leads)
                    values = load(n * UNROLL + (first_ + lowest), UNROLL + max(leads) - lowest)
                for k in range(UNROLL):
                    one(n * UNROLL + (first_ + k), (first_ + k) % 2, lambda lead, k=k: values[k + lead - lowest])
            peeled(range(first_ + UNROLL * loops, TILES + 1))

        def turn(tile, par):
            return (tile - par) // 2 if isinstance(tile, int) else (tile - par) // 2

        with nc.Block() as block:
            @block.sync
            def _(sp):
                sp.wait_ge(experts.planned, 1)
                sp.wait_ge(experts.padded, 16 * (E + 1))

                def stage(name, tile, par, row):
                    if name == "A":
                        if not isinstance(tile, int) or tile >= 2:
                            sp.wait_ge(turned, tile - 1)
                        sp.dma_start(rows_in[par][:], bucket_in[bass.ds(row, P), :]).then_inc(rows_loaded[par], 16)

                run(sp, mybir.EngineType.SP, stage, (("A", 2),), sched_r, "A")

            @block.tensor
            def _(pe):
                pe.wait_ge(experts.planned, 1)
                pe.wait_ge(experts.w1_loaded, 16 * HALVES)
                pe.wait_ge(experts.scaled, HALVES * E)

                def stage(name, tile, par, e):
                    if name == "A":
                        pe.wait_ge(rows_loaded[par], 16 * (turn(tile, par) + 1))
                        if not isinstance(tile, int) or tile >= 2:
                            pe.wait_ge(rows_t_ready, tile - 1)
                        for kk in range(HALVES):
                            last = pe.transpose(xt_ps[par][:, kk * P:(kk + 1) * P], rows_in[par][:, kk * P:(kk + 1) * P], ident[:])
                        last.then_inc(turned, 1)
                    elif name == "B":
                        pe.wait_ge(rows_t_ready, tile + 1)
                        if not isinstance(tile, int) or tile >= 2:
                            pe.wait_ge(hidden_ready, tile - 1)
                        for kk in range(HALVES):
                            last = pe.matmul(h_ps[par][:], rows_t[par][:, kk, :],
                                             w1[:, bass.ds(e, 1), kk * 2 * F:(kk + 1) * 2 * F].rearrange("p o f -> p (o f)"),
                                             start=kk == 0, stop=kk == 1)
                        last.then_inc(first_done, 1)
                    elif name == "C":
                        pe.wait_ge(acts_ready, tile + 1)
                        if not isinstance(tile, int) or tile >= 2:
                            pe.wait_ge(acts_t_ready, tile - 1)
                        for kk in range(HALVES):
                            last = pe.transpose(at_ps[par][:, kk * P:(kk + 1) * P], acts[par][:, kk * P:(kk + 1) * P], ident[:])
                        last.then_inc(acts_turned, 1)
                    else:
                        pe.wait_ge(acts_t_ready, tile + 1)
                        if not isinstance(tile, int) or tile >= 2:
                            pe.wait_ge(out_ready, tile - 1)
                        for kk in range(HALVES):
                            last = pe.matmul(o_ps[par][:, 0:C], acts_t[par][:, kk, :],
                                             w2[:, bass.ds(e, 1), kk * C:(kk + 1) * C].rearrange("p o f -> p (o f)"),
                                             start=kk == 0, stop=kk == 1)
                        last.then_inc(second_done, 1)

                run(pe, mybir.EngineType.PE, stage, (("A", 2), ("C", 0), ("D", -1), ("B", 2)), sched_e, "BD")

            @block.scalar
            def _(act):
                def stage(name, tile, par, e):
                    if name == "A":
                        act.wait_ge(turned, tile + 1)
                        if not isinstance(tile, int) or tile >= 2:
                            act.wait_ge(first_done, tile - 1)
                        act.activation(rows_t[par][:], xt_ps[par][:, 0:C].rearrange("p (k t) -> p k t", k=HALVES), ACT.Copy
                                       ).then_inc(rows_t_ready, 1)
                    elif name == "B":
                        act.wait_ge(hidden_ready, tile + 1)
                        if not isinstance(tile, int) or tile >= 2:
                            act.wait_ge(acts_ready, tile - 1)
                        act.activation(gelu[par][:], hidden[par][:, F:2 * F], ACT.Gelu).then_inc(gelu_ready, 1)
                    elif name == "C":
                        act.wait_ge(acts_turned, tile + 1)
                        if not isinstance(tile, int) or tile >= 2:
                            act.wait_ge(second_done, tile - 1)
                        act.activation(acts_t[par][:], at_ps[par][:, 0:F].rearrange("p (k t) -> p k t", k=HALVES), ACT.Copy
                                       ).then_inc(acts_t_ready, 1)
                    else:
                        row = ahead(act, tile * P)
                        act.wait_ge(out_ready, tile + 1)
                        act.dma_start(tile_out[bass.ds(row, P), :], rows_out[par][:]).then_inc(rows_stored[par], 16)

                act.wait_ge(experts.planned, 1)
                run(act, mybir.EngineType.Activation, stage, (("A", 2), ("C", 0), ("B", 1), ("D", -1)), None, "")
                act.wait_ge(rows_stored[0], 16 * ((TILES + 1) // 2))
                act.wait_ge(rows_stored[1], 16 * (TILES // 2))

            @block.vector
            def _(dve):
                dve.wait_ge(experts.planned, 1)
                dve.wait_ge(experts.biases_loaded, 16 * 2)

                def stage(name, tile, par, e):
                    if name == "B":
                        dve.wait_ge(first_done, tile + 1)
                        dve.tensor_tensor(hidden[par][:], h_ps[par][:], b1[:, bass.ds(e, 1), :].rearrange("p o f -> p (o f)"),
                                          ALU.add).then_inc(hidden_ready, 1)
                        dve.wait_ge(gelu_ready, tile + 1)
                        if not isinstance(tile, int) or tile >= 2:
                            dve.wait_ge(acts_turned, tile - 1)
                        dve.tensor_tensor(acts[par][:], gelu[par][:], hidden[par][:, 0:F], ALU.mult).then_inc(acts_ready, 1)
                    elif name == "D":
                        dve.wait_ge(second_done, tile + 1)
                        if not isinstance(tile, int) or tile >= 2:
                            dve.wait_ge(rows_stored[par], 16 * turn(tile, par))
                        dve.tensor_tensor(rows_out[par][:], o_ps[par][:, 0:C], b2[:, bass.ds(e, 1), :].rearrange("p o f -> p (o f)"),
                                          ALU.add).then_inc(out_ready, 1)

                run(dve, mybir.EngineType.DVE, stage, (("B", 1), ("D", -1)), sched_e, "BD")


def phase3(nc, sb_all, sem, column, weight, slot, rows, s_fc1, s_fc2, x1_dram, x1t_dram, tile_out, out):
    with ExitStack() as ctx:
        def sb(name, shape, dt=F32):
            return sb_all(name, shape, dt, ctx)

        def ps(name, shape, dt=F32):
            return ctx.enter_context(nc.psum_tensor(name, shape, dt))

        M = FS // P
        w1 = sb("sw1", [P, HALVES, 2 * FS])
        w2 = sb("sw2", [P, M, C])
        b2 = sb("sb2", [P, C])
        xt = [sb(f"s_xt{i}", [P, HALVES, T]) for i in range(2)]
        xr = [sb(f"s_xr{i}", [P, Q, C]) for i in range(2)]
        chosen_rows = [sb(f"chosen_rows{i}", [P, Q * TOPK, C]) for i in range(2)]
        slots = [sb(f"slots{i}", [P, Q * TOPK], U32) for i in range(2)]
        wts = [sb(f"wts{i}", [P, Q * TOPK]) for i in range(2)]
        gelu = [sb(f"s_gelu{i}", [P, T]) for i in range(2)]
        acts = [sb(f"s_acts{i}", [P, M, T]) for i in range(2)]
        acc = sb("acc", [P, Q, C])
        bn = sb("s_bn", [P, Q, 6])
        mv = sb("s_mv", [P, Q, 2])
        ln = sb("s_ln", [P, 5, Q])
        result = [sb(f"result{i}", [P, Q, C]) for i in range(2)]
        gx = [[ps(f"ps_s{n}{i}", [P, T]) for i in range(2)] for n in "gx"]
        o_ps = [ps(f"ps_so{i}", [P, T]) for i in range(4)]

        loaded = sem("s_loaded")
        scaled = sem("s_scaled")
        xt_loaded = [sem(f"s_xt_loaded{i}") for i in range(2)]
        xr_loaded = [sem(f"s_xr_loaded{i}") for i in range(2)]
        slots_ready = sem("s_slots_ready")
        gathered = [sem(f"gathered{i}") for i in range(2)]
        g_done = sem("s_g_done")
        gelu_ready = sem("s_gelu_ready")
        acts_ready = sem("s_acts_ready")
        out_done = [sem(f"s_out_done{i}") for i in range(2)]
        acc_step = sem("acc_step")
        taken = sem("s_taken")
        biased = sem("biased")
        picked = sem("s_picked")
        result_ready = sem("result_ready")
        stored = [sem(f"stored{i}") for i in range(2)]
        ACC_STEPS = Q * TOPK + 2 * Q + RSQRT_STEPS

        def run(eng, body):
            with eng.Fori(0, B // 2) as n:
                for par in range(2):
                    body(n * 2 + par, n, par)

        with nc.Block() as block:
            @block.sync
            def _(sp):
                sp.dma_start(w1[:], s_fc1.rearrange("(h p) n -> p h n", p=P)).then_inc(loaded, 16)
                sp.dma_start(w2[:], s_fc2.rearrange("(m p) n -> p m n", p=P)).then_inc(loaded, 16)
                sp.dma_start(b2[:], rows[0:1, E * (2 * F + C):E * (2 * F + C) + C].partition_broadcast(P)
                             .rearrange("p o n -> p (o n)")).then_inc(loaded, 16)

                def load_columns(j, par, waits=()):
                    j = ahead(sp, j)
                    for used, value in [(used, sp.to_reg(value)) for used, value in waits]:
                        sp.wait_ge(used, value)
                    sp.dma_start(xt[par][:].rearrange("p h t -> p (h t)"), x1t_dram[bass.ds(j, 1), :, :]
                                 .rearrange("o p c -> (o p) c")).then_inc(xt_loaded[par], 16)

                def load_rows(j, par, waits=()):
                    at = ahead(sp, j * T)
                    for used, value in [(used, sp.to_reg(value)) for used, value in waits]:
                        sp.wait_ge(used, value)
                    sp.dma_start(xr[par][:], x1_dram[bass.ds(at, T), :].rearrange("(q p) c -> p q c", p=P)
                                 ).then_inc(xr_loaded[par], 16)

                for par in range(2):
                    load_columns(par, par)
                    load_rows(par, par)
                with sp.Fori(1, B // 2) as n:
                    for par in range(2):
                        j = n * 2 + par
                        load_columns(j, par, ((g_done, (j - 1) * M),))
                        load_rows(j, par, ((taken, (j - 1) * 2),))

            @block.gpsimd
            def _(pool):
                def body(j, n, par):
                    wait_apart(pool, (scaled, M), (slots_ready, j + 1))
                    for i in range(Q * TOPK):
                        pool.indirect_dma_start(out=chosen_rows[par][:, i, :], out_offset=None, in_=tile_out,
                                                in_offset=bass.IndirectOffsetOnAxis(ap=slots[par][:, i:i + 1], axis=0)
                                                ).then_inc(gathered[par], 16)
                run(pool, body)

            @block.tensor
            def _(pe):
                pe.wait_ge(loaded, 16 * 3)
                pe.wait_ge(scaled, M)

                def first(j, n, par):
                    pe.wait_ge(xt_loaded[par], 16 * (n + 1))
                    for m in range(M):
                        if m >= 2:
                            pe.wait_ge(acts_ready, j * M + m - 1)
                        elif not isinstance(j, int) or j > 0:
                            pe.wait_ge(acts_ready, j * M + m - 1)
                        for i, at in ((0, FS), (1, 0)):
                            for kk in range(HALVES):
                                last = pe.matmul(gx[i][m % 2][:], w1[:, kk, at + m * P:at + (m + 1) * P], xt[par][:, kk, :],
                                                 start=kk == 0, stop=kk == 1)
                        last.then_inc(g_done, 1)

                def second(j, n, par):
                    pe.wait_ge(acts_ready, (j + 1) * M)
                    for i in range(2):
                        if not isinstance(j, int) or j >= 2:
                            pe.wait_ge(taken, (j - 2) * 2 + i + 1)
                        for q in (2 * i, 2 * i + 1):
                            for m in range(M):
                                last = pe.matmul(o_ps[2 * par + i][:, q % 2 * C:(q % 2 + 1) * C], acts[par][:, m, q * P:(q + 1) * P],
                                                 w2[:, m, :], start=m == 0, stop=m == M - 1)
                        last.then_inc(out_done[i], 1)

                first(0, 0, 0)
                first(1, 0, 1)
                second(0, 0, 0)

                def pair(n):
                    first(n * 2, n, 0)
                    second(n * 2 - 1, n, 1)
                    first(n * 2 + 1, n, 1)
                    second(n * 2, n, 0)

                pair(1)
                with pe.Fori(2, B // 2) as n:
                    pair(n)
                second(B - 1, B // 2 - 1, 1)

            @block.scalar
            def _(act):
                act.wait_ge(scaled, M)

                def body(j, n, par):
                    for m in range(M):
                        act.wait_ge(g_done, j * M + m + 1)
                        act.activation(gelu[m % 2][:], gx[0][m % 2][:], ACT.Gelu, bias=column("s_b1", M + m)).then_inc(gelu_ready, 1)

                def store(j, n, par):
                    act.wait_ge(result_ready, j + 1)
                    act.dma_start(out[bass.ds(j * T, T), :].rearrange("(q p) c -> p q c", p=P), result[par][:]
                                  ).then_inc(stored[par], 16)

                body(0, 0, 0)
                body(1, 0, 1)
                with act.Fori(1, B // 2) as n:
                    for par in range(2):
                        body(n * 2 + par, n, par)
                        store(n * 2 + par - 2, n - 1, par)
                for par in range(2):
                    store(B - 2 + par, B // 2 - 1, par)
                for par in range(2):
                    act.wait_ge(stored[par], 16 * (B // 2))

            @block.vector
            def _(dve):
                chain = Chain(acc_step, ACC_STEPS)
                dve.wait_ge(loaded, 16 * 3)
                for m in range(M):
                    dve.tensor_scalar(w2[:, m, :], w2[:, m, :], column("s_mult", m), None, ALU.mult).then_inc(scaled, 1)

                def pick(j, n, par):
                    if not isinstance(j, int) or j >= 2:
                        dve.wait_ge(gathered[par], 16 * Q * TOPK * n)
                        dve.wait_ge(result_ready, j - 1)
                    dve.tensor_copy(wts[par][:], weight[:, bass.ds(j * Q, Q), :].rearrange("p q k -> p (q k)")).then_inc(picked, 1)
                    dve.tensor_copy(slots[par][:], slot[:, bass.ds(j * Q, Q), :].rearrange("p q k -> p (q k)")
                                    ).then_inc(slots_ready, 1)

                def value(j, n, par, m):
                    dve.wait_ge(gelu_ready, j * M + m + 1)
                    dve.scalar_tensor_tensor(acts[par][:, m, :], gx[1][m % 2][:], column("s_b1", m), gelu[m % 2][:],
                                             ALU.add, ALU.mult).then_inc(acts_ready, 1)

                def sums(j, n, par, piece):
                    if piece == 0:
                        chain.start(j)
                        dve.wait_ge(xr_loaded[par], 16 * (n + 1))
                        if not isinstance(j, int) or j >= 1:
                            dve.wait_ge(result_ready, j)
                        dve.tensor_tensor(acc[:], xr[par][:], b2[:].unsqueeze(1).to_broadcast([P, Q, C]), ALU.add).then_inc(biased, 1)
                        dve.wait_ge(biased, j + 1)
                        for i in range(2):
                            dve.wait_ge(out_done[i], j + 1)
                            dve.tensor_tensor(acc[:, 2 * i:2 * i + 2, :], o_ps[2 * par + i][:].rearrange("p (q c) -> p q c", q=2),
                                              acc[:, 2 * i:2 * i + 2, :], ALU.add).then_inc(taken, 1)
                    elif piece < M - 1:
                        if piece == 1:
                            dve.wait_ge(taken, 2 * j + 2)
                            dve.wait_ge(gathered[par], 16 * Q * TOPK * (n + 1))
                            dve.wait_ge(picked, j + 1)
                        for k in ((0, 1), (2,))[piece - 1]:
                            for q in range(Q):
                                i = q * TOPK + k
                                chain.did(dve.scalar_tensor_tensor(acc[:, q, :], chosen_rows[par][:, i, :], wts[par][:, i:i + 1],
                                                                   acc[:, q, :], ALU.mult, ALU.add))
                            chain.wait(dve)
                        if piece == M - 2:
                            for q in range(Q):
                                chain.did(dve.bn_stats(bn[:, q, :], acc[:, q, :]))
                    else:
                        chain.wait_apart(dve, (scaled, M))
                        for q in range(Q):
                            chain.did(dve.bn_aggr(mv[:, q, :], bn[:, q, :]))
                        chain.wait(dve)
                        rsqrt(dve, chain, ln[:, 0, :], ln[:, 1, :], ln[:, 2, :], ln[:, 3, :], mv[:, :, 1], 1.0, LN_EPS)
                        chain.wait(dve)
                        chain.end()
                        if not isinstance(j, int) or j >= 2:
                            dve.wait_ge(stored[par], 16 * n)
                        for q in range(Q):
                            ins = dve.tensor_scalar(result[par][:, q, :], acc[:, q, :], mv[:, q, 0:1], ln[:, 0, q:q + 1],
                                                    ALU.subtract, ALU.mult)
                        ins.then_inc(result_ready, 1)

                def body(j, n, par, before):
                    for m in range(M):
                        value(j, n, par, m)
                        if before is not None:
                            sums(before, n - 1, par, m)
                    if before is not None:
                        pick(j, n, par)

                assert M == 4
                for par in range(2):
                    pick(par, 0, par)
                for par in range(2):
                    body(par, 0, par, None)
                for par in range(2):
                    body(2 + par, 1, par, par)
                with dve.Fori(2, B // 2) as n:
                    for par in range(2):
                        body(n * 2 + par, n, par, n * 2 + (par - 2))
                for par in range(2):
                    for m in range(M):
                        sums(B - 2 + par, B // 2 - 1, par, m)


def lay_out(a):
    def halves(v):
        return np.asarray(v).reshape(-1, P).T

    cols = np.concatenate([halves(a["L0_attn_miu_x"]), halves(a["L0_attn_lambda_"]), halves(a["L0_attn_td_miu"]),
                           halves(a["L0_attn_u"]), halves(a["L0_attn_gn_gamma"]), halves(a["L0_attn_gn_beta"]),
                           halves(a["L0_ffn_s_fc1_b"]), halves(a["L0_ffn_s_geglu_mult"]), halves(a["L0_ffn_geglu_mult"])], axis=1)
    rows = np.concatenate([np.asarray(a[n]).reshape(-1) for n in ("L0_ffn_fc1_b", "L0_ffn_fc2_b", "L0_ffn_s_fc2_b")])
    arrays = {
        "x": np.asarray(a["L0_attn_x"]).reshape(B * T, C), "cols": cols, "rows": rows.reshape(1, -1),
        "wk": a["L0_attn_Wk"].T, "wv": a["L0_attn_Wv"].T, "wr": a["L0_attn_Wr"].T, "wg": a["L0_attn_Wg"].T,
        "wo": a["L0_attn_Wo"].T, "a_lora": a["L0_attn_A_lora"],
        "b_lora": np.asarray(a["L0_attn_B_lora"]).reshape(5 * LORA, C), "td_a": a["L0_attn_td_A"],
        "td_b": a["L0_attn_td_B"], "gate": a["L0_ffn_gate_w"].T,
        "fc1": np.asarray(a["L0_ffn_fc1_w"]).transpose(0, 2, 1), "fc2": np.asarray(a["L0_ffn_fc2_w"]).transpose(0, 2, 1),
        "s_fc1": a["L0_ffn_s_fc1_w"].T, "s_fc2": a["L0_ffn_s_fc2_w"].T,
    }
    return {k: np.ascontiguousarray(v) for k, v in arrays.items()}


_OUTS = [((B, T, C), "float32")]


def kernel(**inputs):
    import concourse.bacc as bacc
    from concourse.bass_utils import run_bass_kernel_spmd as run

    nc = bacc.Bacc("TRN2", target_bir_lowering=False, num_devices=1)
    arrays = {f"in_{k}": v for k, v in lay_out(inputs).items()}
    args = {k[3:]: nc.dram_tensor(k, v.shape, mybir.dt.from_np(v.dtype), kind="ExternalInput").ap()
            for k, v in arrays.items()}
    out = nc.dram_tensor("out", (B * T, C), F32, kind="ExternalOutput").ap()
    build_program(nc, out=out, **args)
    result = run(nc, [arrays], core_ids=[0])
    return result.results[0]["out"].reshape(B, T, C)
```
